# Optimizing a Trainium2 kernel written in Bass

```python
import numpy as np
import jax
import jax.numpy as jnp

def _softmax(x, axis=-1):
    return jax.nn.softmax(x, axis=axis)

def _gelu(x):
    return jax.nn.gelu(x, approximate=True)

def _silu(x):
    return jax.nn.silu(x)

def _sigmoid(x):
    return jax.nn.sigmoid(x)

def _layernorm(x, axis=-1, eps=1e-05):
    m = jnp.mean(x, axis=axis, keepdims=True)
    v = jnp.var(x, axis=axis, keepdims=True)
    return (x - m) / jnp.sqrt(v + eps)

def _scatter_add(tgt, idx, src, axis=0):
    return tgt.at[idx].add(src)

def _segment_sum(src, seg, n):
    return jax.ops.segment_sum(src, seg, n)
kernel_name = 'mk_gnn_preln_d2_gnn_r16_14cde9'

def setup_inputs(seed: int=0):
    np.random.seed(seed)
    _w = jnp.asarray

    def _rec_inputs():
        import jax
        import jax.numpy as jnp
        _gk = jax.random.key(seed)
        x = -0.0003713 + 1 * jax.random.normal(jax.random.fold_in(_gk, 1), (3125, 256), jnp.float32)
        _s = jax.random.randint(jax.random.fold_in(_gk, 2), (50000,), 0, 3125, jnp.int32)
        _d = jax.random.randint(jax.random.fold_in(_gk, 3), (50000,), 0, 3125, jnp.int32)
        _loop = jnp.arange(3125, dtype=jnp.int32)
        src = jnp.concatenate([_s, _d, _loop])
        dst = jnp.concatenate([_d, _s, _loop])
        _o = jnp.argsort(dst, stable=True)
        src = src[_o]
        dst = dst[_o]
        edge_type_16 = jax.random.randint(jax.random.fold_in(_gk, 13), (103125,), 0, 16, jnp.int32)
        return (x, src, dst, edge_type_16)
    x, src, dst, edge_type_16 = _rec_inputs()

    def _L0_gnn_setup():
        import jax, jax.numpy as jnp
        import numpy as np
        N = 3125
        E = 50000
        D = 256
        key = jax.random.key(seed)
        ks = jax.random.split(key, 8)
        s = 1.0 / np.sqrt(D)
        x = jax.random.normal(ks[0], (N, D), dtype=jnp.float32)
        edge_index = jax.random.randint(ks[1], (2, E), 0, N, dtype=jnp.int64)
        W1 = jax.random.normal(ks[2], (D, D), dtype=jnp.float32) * s
        b1 = jnp.zeros((D,), dtype=jnp.float32)
        W2 = jax.random.normal(ks[3], (D, D), dtype=jnp.float32) * s
        b2 = jnp.zeros((D,), dtype=jnp.float32)
        W3 = jax.random.normal(ks[4], (D, D), dtype=jnp.float32) * s
        b3 = jnp.zeros((D,), dtype=jnp.float32)
        return {'x': x, 'edge_index': edge_index, 'W1': W1, 'b1': b1, 'W2': W2, 'b2': b2, 'W3': W3, 'b3': b3}
    _L0_gnn_all = _L0_gnn_setup()
    _L0_gnn_in = {k: v for k, v in _L0_gnn_all.items() if k in ('W1', 'b1', 'W2', 'b2', 'W3', 'b3')}
    del _L0_gnn_all

    def _L1_gnn_setup():
        import jax, jax.numpy as jnp
        import numpy as np
        N_NODES = 3125
        N_EDGES = 50000
        HDIM = 256
        NUMRELS = 16

        def _gru_cell(x, h, w_ih, w_hh, b_ih, b_hh):
            gi = x @ w_ih.T + b_ih
            gh = h @ w_hh.T + b_hh
            i_r, i_z, i_n = jnp.split(gi, 3, axis=-1)
            h_r, h_z, h_n = jnp.split(gh, 3, axis=-1)
            r = jax.nn.sigmoid(i_r + h_r)
            z = jax.nn.sigmoid(i_z + h_z)
            n = jnp.tanh(i_n + r * h_n)
            return (1.0 - z) * n + z * h
        key = jax.random.key(seed)
        ks = jax.random.split(key, 9)
        h = jax.random.normal(ks[0], (N_NODES, HDIM), dtype=jnp.float32)
        relvectors = jax.random.normal(ks[1], (NUMRELS, HDIM), dtype=jnp.float32)
        s = 1.0 / np.sqrt(HDIM)
        w_ih = jax.random.uniform(ks[2], (3 * HDIM, HDIM), minval=-s, maxval=s, dtype=jnp.float32)
        w_hh = jax.random.uniform(ks[3], (3 * HDIM, HDIM), minval=-s, maxval=s, dtype=jnp.float32)
        b_ih = jax.random.uniform(ks[4], (3 * HDIM,), minval=-s, maxval=s, dtype=jnp.float32)
        b_hh = jax.random.uniform(ks[5], (3 * HDIM,), minval=-s, maxval=s, dtype=jnp.float32)
        edge_src = jax.random.randint(ks[6], (N_EDGES,), 0, N_NODES, dtype=jnp.int32)
        edge_dst = jax.random.randint(ks[7], (N_EDGES,), 0, N_NODES, dtype=jnp.int32)
        edge_rel = jax.random.randint(ks[8], (N_EDGES,), 0, NUMRELS, dtype=jnp.int32)
        return {'h': h, 'relvectors': relvectors, 'w_ih': w_ih, 'w_hh': w_hh, 'b_ih': b_ih, 'b_hh': b_hh, 'edge_src': edge_src, 'edge_dst': edge_dst, 'edge_rel': edge_rel}
    _L1_gnn_all = _L1_gnn_setup()
    _L1_gnn_in = {k: v for k, v in _L1_gnn_all.items() if k in ('relvectors', 'w_ih', 'w_hh', 'b_ih', 'b_hh')}
    del _L1_gnn_all
    return {'x': x, 'src': src, 'dst': dst, 'edge_type_16': edge_type_16, 'L0_gnn_W1': _L0_gnn_in['W1'], 'L0_gnn_b1': _L0_gnn_in['b1'], 'L0_gnn_W2': _L0_gnn_in['W2'], 'L0_gnn_b2': _L0_gnn_in['b2'], 'L0_gnn_W3': _L0_gnn_in['W3'], 'L0_gnn_b3': _L0_gnn_in['b3'], 'L1_gnn_relvectors': _L1_gnn_in['relvectors'], 'L1_gnn_w_ih': _L1_gnn_in['w_ih'], 'L1_gnn_w_hh': _L1_gnn_in['w_hh'], 'L1_gnn_b_ih': _L1_gnn_in['b_ih'], 'L1_gnn_b_hh': _L1_gnn_in['b_hh']}

def reference(x, src, dst, edge_type_16, L0_gnn_W1, L0_gnn_b1, L0_gnn_W2, L0_gnn_b2, L0_gnn_W3, L0_gnn_b3, L1_gnn_relvectors, L1_gnn_w_ih, L1_gnn_w_hh, L1_gnn_b_ih, L1_gnn_b_hh):
    import jax
    import jax.numpy as jnp

    def _L0_gnn_ref(x, edge_index, W1, b1, W2, b2, W3, b3):
        import jax, jax.numpy as jnp
        import numpy as np
        N = 3125
        E = 50000
        D = 256
        n = x.shape[0]
        loop = jnp.arange(n, dtype=edge_index.dtype)
        src = jnp.concatenate([edge_index[0], loop])
        dst = jnp.concatenate([edge_index[1], loop])
        deg = jax.ops.segment_sum(jnp.ones_like(src, dtype=x.dtype), dst, num_segments=n)
        dinv = jnp.where(deg > 0, jax.lax.rsqrt(deg), 0.0)
        norm = (dinv[src] * dinv[dst])[:, None]

        def conv(h, W, b):
            h = h @ W
            agg = jax.ops.segment_sum(h[src] * norm, dst, num_segments=n)
            return agg + b
        h = jax.nn.relu(conv(x, W1, b1))
        h = jax.nn.relu(conv(h, W2, b2))
        return conv(h, W3, b3)

    def _L1_gnn_ref(h, relvectors, w_ih, w_hh, b_ih, b_hh, edge_src, edge_dst, edge_rel):
        import jax, jax.numpy as jnp
        import numpy as np
        N_NODES = 3125
        N_EDGES = 50000
        HDIM = 256
        NUMRELS = 16

        def _gru_cell(x, h, w_ih, w_hh, b_ih, b_hh):
            gi = x @ w_ih.T + b_ih
            gh = h @ w_hh.T + b_hh
            i_r, i_z, i_n = jnp.split(gi, 3, axis=-1)
            h_r, h_z, h_n = jnp.split(gh, 3, axis=-1)
            r = jax.nn.sigmoid(i_r + h_r)
            z = jax.nn.sigmoid(i_z + h_z)
            n = jnp.tanh(i_n + r * h_n)
            return (1.0 - z) * n + z * h
        msg = h[edge_src] + relvectors[edge_rel]
        red = jax.ops.segment_sum(msg, edge_dst, num_segments=h.shape[0])
        return _gru_cell(red, h, w_ih, w_hh, b_ih, b_hh)
    edge_index = jnp.stack([src, dst])
    h = jnp.maximum(_layernorm(x, axis=-1), 0.0)
    x = x + _L0_gnn_ref(h, edge_index, L0_gnn_W1, L0_gnn_b1, L0_gnn_W2, L0_gnn_b2, L0_gnn_W3, L0_gnn_b3)
    h = jnp.maximum(_layernorm(x, axis=-1), 0.0)
    x = x + _L1_gnn_ref(h, L1_gnn_relvectors, L1_gnn_w_ih, L1_gnn_w_hh, L1_gnn_b_ih, L1_gnn_b_hh, src, dst, edge_type_16)
    return x

_drawn_inputs = setup_inputs


def setup_inputs(seed=0):
    import zlib

    import numpy as np

    out = dict(_drawn_inputs(seed))
    spreads = {'L0_gnn_b1': (0.0, 0.1), 'L0_gnn_b2': (0.0, 0.1), 'L0_gnn_b3': (0.0, 0.1)}
    factors = {'L1_gnn_b_ih': 8.0, 'L1_gnn_b_hh': 8.0}
    for name, (base, spread) in spreads.items():
        noise = np.random.default_rng([zlib.crc32(name.encode()), seed]).standard_normal(out[name].shape)
        drawn = base * np.exp(spread * noise) if base else spread * noise
        out[name] = jnp.asarray(drawn.astype(out[name].dtype))
    for name, factor in factors.items():
        out[name] = (out[name] * factor).astype(out[name].dtype)
    return out
```

```python
from contextlib import ExitStack

import concourse.bass as bass
from concourse import mybir

ALU = mybir.AluOpType
ACT = mybir.ActivationFunctionType
AX_X = mybir.AxisListType.X
F32, F16, I32 = mybir.dt.float32, mybir.dt.float16, mybir.dt.int32
RADD = bass.bass_isa.ReduceOp.add
RMAX = bass.bass_isa.ReduceOp.max

P = 128
EPS = 1e-5
BANK = 512
SUPER = 2 * P
WINDOW = 12
BATCH = 4
SMALL = 8
REL_ROW = 64
RING = 8
AGG_RING = 3
LOADS = 16


class Stream:

    def __init__(self, ctx, nc, name, by=1):
        self.sem, self.by, self.n = ctx.enter_context(nc.semaphore(name)), by, 0

    def mark(self, instruction):
        instruction.then_inc(self.sem, self.by)
        self.n += self.by
        return self.sem, self.n

    @property
    def last(self):
        return self.sem, self.n


def wait(engine, *marks):
    for sem, value in marks:
        engine.wait_ge(sem, value)


def program(nc, x, src, dst, rel, convs, relvec, w_ih_t, w_hh_t, b_ih, b_hh, x1_dram, table_dram, out):
    N, D = x.shape
    E = src.shape[0]
    R = relvec.shape[0]
    T = -(-N // P)
    TAIL = N - (T - 1) * P
    NS = -(-E // SUPER)
    Q = -(-NS // P)
    FULL = E // SUPER
    LEFT = E - FULL * SUPER
    KEYS = T * WINDOW
    CW = N + WINDOW - 1
    HALVES = D // P
    G = 3 * D
    CHUNK = BANK
    NC = -(-N // CHUNK)
    assert RING == 2 * BATCH and D == 2 * P and FULL == NS - 1 and 2 * LEFT >= SUPER and TAIL <= REL_ROW - 11 and R <= 16 and NS > 7
    SP, PE, DVE, ACTE, POOL = nc.sync, nc.tensor, nc.vector, nc.scalar, nc.gpsimd

    def rows(t):
        return P if t < T - 1 else TAIL

    with ExitStack() as ctx:
        def sb(name, shape, dt):
            return ctx.enter_context(nc.sbuf_tensor(name, shape, dt))

        def stream(name, by=1):
            return Stream(ctx, nc, name, by)

        count = sb("count", [P, T, CW], F16)
        node_a = sb("node_a", [P, T, 2, D], F16)
        node_b = sb("node_b", [P, T, 2, D], F16)
        weight = [sb(f"weight{i}", [P, HALVES, D], F32) for i in range(2)]
        bias = [sb(f"bias{i}", [P, D], F32) for i in range(3)]
        agg = sb("agg", [P, HALVES, CHUNK], F32)
        work = [sb(f"work{i}", [P, D], F32) for i in range(2)]
        scaled = [sb(f"scaled{i}", [P, D], F32) for i in range(2)]
        xt = [sb(f"xt{i}", [P, D], F32) for i in range(2)]
        ident = sb("ident", [P, P], F32)
        ident16 = sb("ident16", [P, P], F16)
        ones16 = sb("ones16", [P, 1], F16)
        stats = sb("stats", [P, 2, 6], F32)
        moments = sb("moments", [P, T, 2], F32)
        rstd = sb("rstd", [P, T], F32)
        negmr = sb("negmr", [P, T], F32)
        dinv = sb("dinv", [P, T], F32)
        dscale = sb("dscale", [P, T], F32)
        newt = sb("newt", [P, 4, T], F32)
        fours = sb("fours", [P, 8], F32)
        bounds = sb("bounds", [P, 8], F32)
        scales = sb("scales", [P, 8], F32)
        verdict = sb("verdict", [P, 1], F32)
        verdict_i = sb("verdict_i", [1, 1], I32)

        flat = count[:, :, :].rearrange("p t c -> p (t c)")
        at = [0]

        def early(n, dt=F32):
            words = flat[:, at[0]:at[0] + 2 * n]
            at[0] += 2 * n
            return words.bitcast(dt)

        src_row, dst_row, rel_row, high_row, low_row = (
            early(Q * SUPER, I32).rearrange("p (q e) -> p q e", q=Q) for _ in range(5))
        low_r, key_r, rel_r, rank_r = (early(Q * SUPER // 2).bitcast(F16).rearrange("p (q e) -> p q e", q=Q)
                                       for _ in range(4))
        next_row = early(Q, I32)
        chain = early(NS + 1)
        ones = early(P)
        iota_i = early(2 * KEYS, I32)
        start_f = early(NS + 1)
        rules = early(2 * Q + 3 * Q + 4)
        assert at[0] <= T * CW

        h1 = node_b[:, :, :, :].rearrange("p t a d -> p (t a d)").bitcast(F32).rearrange("p (t d) -> p t d", t=T)

        flat_a = node_a[:, :, :, :].rearrange("p t a d -> p (t a d)")
        at_a = [0]

        def while_counting(n, dt=F16):
            size = n if dt == F16 else 2 * n
            words = flat_a[:, at_a[0]:at_a[0] + size]
            at_a[0] += size
            return words if dt == F16 else words.bitcast(dt)

        iota2 = while_counting(2 * KEYS)
        low_k, key_k, rel_k, rank_k = (while_counting(2 * NS) for _ in range(4))
        starts = while_counting(NS + 1, I32)[0:1, :]
        key_hot = [while_counting(BATCH * KEYS * 2).rearrange("p (s k j) -> p s k j", s=BATCH, j=2) for _ in range(2)]
        low_hot = [while_counting(BATCH * P * 2).rearrange("p (s k j) -> p s k j", s=BATCH, j=2) for _ in range(2)]
        rel_hot = [while_counting(SMALL * R * 2).rearrange("p (s k j) -> p s k j", s=SMALL, j=2) for _ in range(2)]
        rank_hot = [while_counting(SMALL * WINDOW * 2).rearrange("p (s k j) -> p s k j", s=SMALL, j=2)
                    for _ in range(2)]
        assert at_a[0] <= T * 2 * D

        ps = ctx.enter_context(nc.psum_tensor("ps", [P, 8, BANK], F32))

        pe, dve, act, pool = stream("pe_done"), stream("dve_done"), stream("act_done"), stream("pool_done")

        def dma(name, engine, to, of, **kw):
            return stream(name, 16).mark(engine.dma_start(to, of, **kw))

        whole = (Q - 1) * P
        rest = FULL - whole
        pads = []
        pads.append(dve.mark(DVE.memset(src_row[:, Q - 1, :], -1)))
        pads.append(dve.mark(DVE.memset(dst_row[:, Q - 1, :], -1)))
        pads.append(dve.mark(DVE.memset(rel_row[:, Q - 1, :], -1)))
        pads.append(dve.mark(DVE.memset(next_row[:, :], N)))
        starts_in = dma("starts", ACTE, starts[:, 0:FULL],
                        dst[0:FULL * SUPER].rearrange("(p s e) -> p s e", p=1, e=SUPER)[:, :, 0],
                        allow_slow_non_contiguous=True)
        starts_last = dma("starts_last", ACTE, starts[:, FULL:NS],
                          dst[FULL * SUPER:FULL * SUPER + 1].rearrange("(p e) -> p e", p=1))
        wait(ACTE, dve.last)
        nexts = [dma("next_full", ACTE, next_row[:, 0:Q - 1],
                     dst[SUPER:(whole + 1) * SUPER].rearrange("(q p e) -> p q e", p=P, e=SUPER)[:, :, 0],
                     allow_slow_non_contiguous=True),
                 dma("next_rest", ACTE, next_row[0:rest, Q - 1:Q],
                     dst[whole * SUPER + 1:FULL * SUPER + 1].rearrange("(p e) -> p e", e=SUPER)[:, SUPER - 1:SUPER],
                     allow_slow_non_contiguous=True)]
        edges_in = {}
        for name, row, of in (("src", src_row, src), ("dst", dst_row, dst), ("rel", rel_row, rel)):
            edges_in[name] = [dma(f"{name}_full", SP, row[:, 0:Q - 1, :],
                                  of[0:whole * SUPER].rearrange("(q p e) -> p q e", p=P, e=SUPER))]
            wait(SP, dve.last)
            edges_in[name].append(dma(f"{name}_rest", SP, row[0:rest, Q - 1, :],
                                      of[whole * SUPER:FULL * SUPER].rearrange("(p e) -> p e", e=SUPER)))
            edges_in[name].append(dma(f"{name}_left", SP, row[rest:rest + 1, Q - 1, 0:LEFT],
                                      of[FULL * SUPER:E].rearrange("(p e) -> p e", p=1)))
        edges_in["dst"].append(dma("dst_pad", SP, dst_row[rest:rest + 1, Q - 1, LEFT:SUPER],
                                   dst[E - (SUPER - LEFT):E].rearrange("(p e) -> p e", p=1)))
        wait(SP, *edges_in["rel"])
        assert (T - 1) % 6 == 0
        x_in = [dma(f"x_in{g}", SP, h1[:, g * 6:g * 6 + 6, :],
                    x[g * 6 * P:(g * 6 + 6) * P, :].rearrange("(t p) d -> p t d", p=P)) for g in range((T - 1) // 6)]
        x_tail = dma("x_tail", SP, h1[0:TAIL, T - 1, :], x[(T - 1) * P:N, :])
        weights_in = [dma(f"w{i}_in", SP, weight[i][:, :, :], convs[i][0].rearrange("(f p) d -> p f d", p=P))
                      for i in range(2)]
        biases_in = [dma(f"b{i}_in", SP, bias[i][:, :],
                         convs[i][1].rearrange("(p d) -> p d", p=1).to_broadcast([P, D])) for i in range(3)]
        rel_in = dma("rel_in", SP, work[0][REL_ROW:REL_ROW + R, :], relvec)

        made = pool.mark(POOL.iota(iota_i[:, :], pattern=[[1, KEYS], [0, 2]], base=0, channel_multiplier=0))
        wait(DVE, made)
        dve.mark(DVE.tensor_copy(iota2[:, :], iota_i[:, :]))
        ident_zero = dve.mark(DVE.memset(ident[:, :], 0.0))
        dve.mark(DVE.memset(ones[:, :], 1.0))
        dve.mark(DVE.memset(ones16[:, :], 1.0))
        dve.mark(DVE.memset(bounds[:, :], 0.0))
        dve.mark(DVE.memset(rules, 0.0))
        dve.mark(DVE.memset(moments[:, :, :], 1.0))
        dve.mark(DVE.memset(newt[:, :, :], 1.0))
        column_ones = xt[0][:, 0:P]
        dve.mark(DVE.memset(column_ones, 1.0))
        wait(POOL, ident_zero)
        ident_in = pool.mark(POOL.affine_select(out=ident[:, :], in_=ident[:, :], compare_op=ALU.not_equal, fill=1.0,
                                                base=0, pattern=[[-1, P]], channel_multiplier=1))
        wait(DVE, ident_in)
        dve.mark(DVE.tensor_copy(ident16[:, :], ident[:, :]))

        row_max, row_min = rules[:, 0:Q], rules[:, Q:2 * Q]
        broken_rows = rules[:, 2 * Q:5 * Q].rearrange("p (r q) -> p r q", q=Q)
        broken_all = rules[:, 5 * Q:5 * Q + 4]
        gap = 7
        wait(DVE, starts_in, starts_last)
        wait(DVE, dve.mark(DVE.tensor_copy(start_f[0:1, 0:NS], starts[:, 0:NS])))
        wait(DVE, dve.mark(DVE.tensor_tensor(chain[0:1, 0:NS - 1], start_f[0:1, 1:NS], start_f[0:1, 0:NS - 1], ALU.subtract)))
        wait(DVE, dve.mark(DVE.tensor_reduce(broken_all[0:1, 0:1], chain[0:1, 0:NS - 1], AX_X, ALU.max)))
        wait(DVE, dve.mark(DVE.tensor_tensor(chain[0:1, 0:NS - gap], start_f[0:1, gap:NS], start_f[0:1, 0:NS - gap], ALU.subtract)))
        wait(DVE, dve.mark(DVE.tensor_reduce(broken_all[0:1, 1:2], chain[0:1, 0:NS - gap], AX_X, ALU.min)))
        dve.mark(DVE.tensor_scalar(broken_all[0:1, 0:1], broken_all[0:1, 0:1], float(WINDOW - 1), None, ALU.is_gt))
        dve.mark(DVE.tensor_scalar(broken_all[0:1, 1:2], broken_all[0:1, 1:2], 1.0, None, ALU.is_lt))
        dve.mark(DVE.tensor_scalar(broken_all[0:1, 2:3], start_f[0:1, 0:1], 0.0, None, ALU.is_gt))
        dve.mark(DVE.tensor_scalar(broken_all[0:1, 3:4], start_f[0:1, NS - 1:NS], float(N - WINDOW), None, ALU.is_lt))

        wait(DVE, *edges_in["src"])
        low_here = dve.mark(DVE.tensor_scalar(low_row, src_row, P - 1, None, ALU.bitwise_and))
        dve.mark(DVE.tensor_scalar(high_row, src_row, 7, None, ALU.arith_shift_right))
        wait(DVE, *edges_in["dst"])
        rank_done = dve.mark(DVE.tensor_tensor(rank_r, dst_row, dst_row[:, :, 0:1].to_broadcast([P, Q, SUPER]), ALU.subtract))
        wait(DVE, rank_done)
        key_done = dve.mark(DVE.scalar_tensor_tensor(out=key_r, in0=high_row, scalar=float(WINDOW), in1=rank_r,
                                                     op0=ALU.mult, op1=ALU.add))
        wait(ACTE, low_here)
        low_done = act.mark(ACTE.activation(low_r, low_row, ACT.Copy))
        wait(ACTE, *edges_in["rel"])
        rel_done = act.mark(ACTE.activation(rel_r, rel_row, ACT.Copy))

        dve.mark(DVE.tensor_reduce(row_max, dst_row, AX_X, ALU.max))
        dve.mark(DVE.tensor_reduce(row_min, dst_row, AX_X, ALU.min))
        wait(DVE, *nexts, dve.last)
        dve.mark(DVE.tensor_tensor(broken_rows[:, 0, :], row_max, dst_row[:, :, 0], ALU.subtract))
        dve.mark(DVE.tensor_tensor(broken_rows[:, 1, :], row_min, dst_row[:, :, 0], ALU.subtract))
        dve.mark(DVE.tensor_tensor(broken_rows[:, 2, :], row_max, next_row, ALU.subtract))
        wait(DVE, dve.last)
        dve.mark(DVE.tensor_scalar(broken_rows[:, 0, :], broken_rows[:, 0, :], float(WINDOW - 1), None, ALU.is_gt))
        dve.mark(DVE.tensor_scalar(broken_rows[:, 1, :], broken_rows[:, 1, :], 0.0, None, ALU.is_lt))
        dve.mark(DVE.tensor_scalar(broken_rows[:, 2, :], broken_rows[:, 2, :], 0.0, None, ALU.is_gt))
        wait(DVE, dve.last)
        broken = dve.mark(DVE.tensor_reduce(verdict[:, :], rules[:, 2 * Q:5 * Q + 4], AX_X, ALU.add))

        turned = []
        for bank, (row, ready) in enumerate(((low_r, low_done), (rank_r, rank_done), (key_r, key_done), (rel_r, rel_done))):
            wait(PE, ready, dve.last if bank == 0 else ready)
            half_bank = ps[:, bank, :].bitcast(F16).rearrange("p (j s) -> p j s", j=2)
            for j in range(2):
                for q in range(Q):
                    last = PE.transpose(half_bank[:, j, q * P:(q + 1) * P], row[:, q, j * P:(j + 1) * P], ident16[:, :])
            turned.append((half_bank[:, :, 0:NS], pe.mark(last)))
        for n, k in ((0, low_k), (3, rel_k)):
            wait(ACTE, turned[n][1])
            act.mark(ACTE.activation(k.rearrange("p (s j) -> p j s", j=2), turned[n][0], ACT.Copy))
        wait(PE, broken)
        judged = pe.mark(PE.matmul(ps[0:1, 4, 0:1], verdict[:, :], ones[:, 0:1], start=True, stop=True))
        for n, k in ((1, rank_k), (2, key_k)):
            wait(DVE, turned[n][1])
            dve.mark(DVE.tensor_copy(k.rearrange("p (s j) -> p j s", j=2), turned[n][0]))
        wait(DVE, judged)
        verdict_in = dve.mark(DVE.tensor_copy(verdict_i[:, :], ps[0:1, 4, 0:1]))
        keys_ready = [act.last, dve.last]

        def root_steps(src_ap, dst_ap, tmp):
            done = []

            def root():
                wait(ACTE, dve.last)
                done.append(act.mark(ACTE.activation(tmp[0], src_ap, ACT.Sqrt)))

            def on_dve(instruction):
                def step():
                    wait(DVE, done[-1])
                    done.append(dve.mark(instruction()))
                return step

            return [root,
                    on_dve(lambda: DVE.reciprocal(tmp[1], tmp[0])),
                    on_dve(lambda: DVE.tensor_tensor(tmp[2], tmp[1], tmp[1], ALU.mult)),
                    on_dve(lambda: DVE.tensor_tensor(tmp[2], tmp[2], src_ap, ALU.mult)),
                    on_dve(lambda: DVE.tensor_scalar(tmp[2], tmp[2], -0.5, 1.5, ALU.mult, ALU.add)),
                    on_dve(lambda: DVE.tensor_tensor(dst_ap, tmp[1], tmp[2], ALU.mult))]

        def inverse_root(src_ap, dst_ap, tmp):
            for step in root_steps(src_ap, dst_ap, tmp):
                step()
            wait(DVE, dve.last)

        def norm_x():
            used, ready = [None, None], {}

            def x_tile_of(t):
                return h1[0:rows(t), t, :]

            def total(t):
                m, k = rows(t), t % 2
                wait(ACTE, x_in[t // 6] if t < T - 1 else x_tail)
                if used[k]:
                    wait(ACTE, used[k])
                used[k] = act.mark(ACTE.activation(scaled[k][0:m, :], x_tile_of(t), ACT.Copy,
                                                   accum_out=newt[0:m, 0, t:t + 1]))

            def mean():
                wait(DVE, *used)
                ready["mean"] = dve.mark(DVE.tensor_scalar(negmr[:, :], newt[:, 0, :], -1.0 / D, None, ALU.mult))

            def squares(t):
                m, k = rows(t), t % 2
                wait(ACTE, used[k], ready["mean"])
                used[k] = act.mark(ACTE.activation(scaled[k][0:m, :], x_tile_of(t), ACT.Square, bias=negmr[0:m, t:t + 1],
                                                   accum_out=newt[0:m, 2, t:t + 1]))

            def variance():
                wait(DVE, *used)
                dve.mark(DVE.tensor_scalar(newt[:, 3, :], newt[:, 2, :], 1.0 / D, EPS, ALU.mult, ALU.add))

            def mean_over_deviation():
                wait(DVE, dve.last)
                ready["norm"] = dve.mark(DVE.tensor_tensor(negmr[:, :], negmr[:, :], rstd[:, :], ALU.mult))

            def pause():
                pass

            def relu(t):
                m = rows(t)
                wait(ACTE, ready["norm"])
                act.mark(ACTE.activation(x_tile_of(t), x_tile_of(t), ACT.Relu, bias=negmr[0:m, t:t + 1],
                                         scale=rstd[0:m, t:t + 1]))

            return [*[lambda t=t: total(t) for t in range(T)], pause, mean, *[lambda t=t: squares(t) for t in range(T)],
                    pause, variance, *root_steps(newt[:, 3, :], rstd[:, :], [newt[:, i, :] for i in range(3)]),
                    mean_over_deviation, *[lambda t=t: relu(t) for t in range(T)]]

        def residual_tile(t, b, done, streams, x_read):
            m, k = rows(t), t % 2
            x_loads, x1_stores = streams
            if k in x_read:
                wait(SP, *x_read[k])
            x_here = x_loads[k].mark(SP.dma_start(xt[k][0:m, :], x[t * P:t * P + m, :]))
            wait(DVE, done, dve.last)
            product_read = dve.mark(DVE.scalar_tensor_tensor(
                out=work[k][0:m, :], in0=ps[0:m, b, 0:D], scalar=dinv[0:m, t:t + 1], in1=bias[2][0:m, :],
                op0=ALU.mult, op1=ALU.add))
            wait(DVE, product_read, x_here)
            x1_here = dve.mark(DVE.tensor_tensor(xt[k][0:m, :], xt[k][0:m, :], work[k][0:m, :], ALU.add))
            wait(ACTE, x1_here)
            stored = x1_stores[k].mark(ACTE.dma_start(x1_dram[t * P:t * P + m, :], xt[k][0:m, :]))
            wait(DVE, x1_here)
            wait(DVE, dve.mark(DVE.bn_stats(stats[0:m, k, :], xt[k][0:m, :])))
            wait(DVE, dve.mark(DVE.bn_aggr(moments[0:m, t, :], stats[0:m, k, :])))
            wait(DVE, dve.mark(DVE.tensor_scalar(newt[0:m, 3, t:t + 1], moments[0:m, t, 1:2], EPS, None, ALU.add)))
            inverse_root(newt[0:m, 3, t:t + 1], rstd[0:m, t:t + 1], [newt[0:m, i, t:t + 1] for i in range(3)])
            wait(DVE, dve.last)
            dve.mark(DVE.scalar_tensor_tensor(out=negmr[0:m, t:t + 1], in0=moments[0:m, t, 0:1], scalar=-1.0,
                                              in1=rstd[0:m, t:t + 1], op0=ALU.mult, op1=ALU.mult))
            x_read[k] = [dve.last, stored]
            return product_read

        def gru_setup(tag, x1_stored, order):
            at_a[0] = 0
            w_ih_sb, w_hh_sb = (while_counting(HALVES * G, F32).rearrange("p (f g) -> p f g", f=HALVES) for _ in range(2))
            bias_rz, bias_rz2 = while_counting(2 * D, F32), while_counting(2 * D, F32)
            bias_in, bias_hn = while_counting(D, F32), while_counting(D, F32)
            h_t = [while_counting(HALVES * P, F32).rearrange("p (f n) -> p f n", f=HALVES) for _ in range(2)]
            gate_rz = [while_counting(2 * D, F32), bias_rz2]
            x1_tile = [xt[0][:, :], xt[1][:, :], while_counting(D, F32)]
            h_tile = [scaled[0][:, :], scaled[1][:, :], while_counting(D, F32)]
            n_tile = work
            AHEAD = len(x1_tile)
            assert at_a[0] <= T * 2 * D
            wait(SP, pe.last, dve.last, act.last, *x1_stored)
            x1_loads = [stream(tag + f"x1_in{k}", 16) for k in range(AHEAD)]
            out_stores = [stream(tag + f"out{k}", 16) for k in range(AHEAD)]

            def load_x1(i):
                t = order[i]
                return x1_loads[i % AHEAD].mark(SP.dma_start(x1_tile[i % AHEAD][0:rows(t), :],
                                                             x1_dram[t * P:t * P + rows(t), :]))

            x1_here = {i: load_x1(i) for i in range(AHEAD)}
            w_gru_in = [dma(tag + "w_ih_in", SP, w_ih_sb, w_ih_t.rearrange("(f p) g -> p f g", p=P)),
                        dma(tag + "w_hh_in", SP, w_hh_sb, w_hh_t.rearrange("(f p) g -> p f g", p=P))]

            def spread(v):
                return v.rearrange("(p d) -> p d", p=1).to_broadcast([P, v.shape[0]])

            b_gru_in = [dma(tag + "b_rz_in", SP, bias_rz, spread(b_ih[0:2 * D])), dma(tag + "b_rz2_in", SP, bias_rz2, spread(b_hh[0:2 * D])),
                        dma(tag + "b_in_in", SP, bias_in, spread(b_ih[2 * D:G])), dma(tag + "b_hn_in", SP, bias_hn, spread(b_hh[2 * D:G]))]
            norms_here = dve.last
            H_BANK, RZ_BANK, N_BANK = 3, (4, 5), (6, 7)
            h_here, h_turned, n_done, n_sum, z_read, result, kept = {}, {}, {}, {}, {}, {}, {}
            bias_here = []

            def make_h(i):
                t, k = order[i], i % AHEAD
                m = rows(t)
                wait(ACTE, x1_here[i], norms_here)
                if i >= AHEAD:
                    wait(ACTE, kept[i - AHEAD])
                h_here[i] = act.mark(ACTE.activation(h_tile[k][0:m, :], x1_tile[k][0:m, :], ACT.Relu,
                                                     bias=negmr[0:m, t:t + 1], scale=rstd[0:m, t:t + 1]))

            def turn_h(i):
                m = rows(order[i])
                wait(PE, h_here[i])
                if i:
                    wait(PE, h_turned[i - 1])
                for f in range(HALVES):
                    turned = pe.mark(PE.transpose(ps[:, H_BANK, f * P:f * P + m], h_tile[i % AHEAD][0:m, f * P:(f + 1) * P],
                                                  ident[0:m, 0:m]))
                wait(ACTE, turned)
                if i >= 2:
                    wait(ACTE, n_done[i - 2])
                h_turned[i] = act.mark(ACTE.activation(
                    h_t[i % 2][:, :, 0:m], ps[:, H_BANK, 0:HALVES * P].rearrange("p (f n) -> p f n", f=HALVES)[:, :, 0:m], ACT.Copy))

            def gru_tile(i, sums, halves):
                t, k, x = order[i], i % 2, i % AHEAD
                m = rows(t)
                if i == 0:
                    make_h(0)
                    turn_h(0)
                    wait(DVE, *b_gru_in)
                    bias_here.append(dve.mark(DVE.tensor_tensor(bias_rz, bias_rz, bias_rz2, ALU.add)))
                if i + 1 < T:
                    make_h(i + 1)
                rz, nn = RZ_BANK[k], N_BANK[k]
                wait(PE, *halves, *w_gru_in, h_turned[i])
                if i >= 2:
                    wait(PE, n_sum[i - 2])
                hs = [h_t[k][:, f, 0:m] for f in range(HALVES)]
                for n, (l, w, f) in enumerate([(sums[f], w_ih_sb, f) for f in range(HALVES)] +
                                              [(hs[f], w_hh_sb, f) for f in range(HALVES)]):
                    done = PE.matmul(ps[0:m, rz, 0:2 * D], l, w[:, f, 0:2 * D], start=(n == 0), stop=(n == 2 * HALVES - 1))
                rz_done = pe.mark(done)
                for col, ls, w in ((0, sums, w_ih_sb), (D, hs, w_hh_sb)):
                    for f in range(HALVES):
                        done = PE.matmul(ps[0:m, nn, col:col + D], ls[f], w[:, f, 2 * D:G], start=(f == 0),
                                         stop=(f == HALVES - 1))
                n_done[i] = pe.mark(done)
                if i + 1 < T:
                    turn_h(i + 1)
                rz_gate, v, h = gate_rz[k], n_tile[k][0:m, :], h_tile[x][0:m, :]
                wait(DVE, rz_done, *bias_here)
                if i >= 2:
                    wait(DVE, z_read[i - 2], result[i - 2])
                biased = dve.mark(DVE.tensor_tensor(rz_gate[0:m, :], ps[0:m, rz, :], bias_rz[0:m, :], ALU.add))
                wait(ACTE, biased)
                gates = act.mark(ACTE.activation(rz_gate[0:m, :], rz_gate[0:m, :], ACT.Sigmoid))
                wait(DVE, n_done[i])
                wait(DVE, dve.mark(DVE.tensor_tensor(v, ps[0:m, nn, D:2 * D], bias_hn[0:m, :], ALU.add)), gates)
                wait(DVE, dve.mark(DVE.tensor_tensor(v, v, rz_gate[0:m, 0:D], ALU.mult)))
                n_sum[i] = dve.mark(DVE.tensor_tensor(v, ps[0:m, nn, 0:D], v, ALU.add))
                wait(DVE, n_sum[i])
                wait(ACTE, dve.mark(DVE.tensor_tensor(v, v, bias_in[0:m, :], ALU.add)))
                new_n = act.mark(ACTE.activation(v, v, ACT.Tanh))
                wait(DVE, new_n)
                wait(DVE, dve.mark(DVE.tensor_tensor(h, h, v, ALU.subtract)))
                z_read[i] = dve.mark(DVE.tensor_tensor(h, h, rz_gate[0:m, D:2 * D], ALU.mult))
                dve.mark(DVE.tensor_tensor(v, v, x1_tile[x][0:m, :], ALU.add))
                wait(DVE, dve.last)
                result[i] = dve.mark(DVE.tensor_tensor(h, h, v, ALU.add))
                wait(SP, result[i])
                kept[i] = out_stores[x].mark(SP.dma_start(out[t * P:t * P + m, :], h))
                if i + AHEAD < T:
                    x1_here[i + AHEAD] = load_x1(i + AHEAD)
                if i == T - 1:
                    wait(SP, *[s.last for s in out_stores])
            return gru_tile

        for engine in (SP, PE, DVE, ACTE, POOL):
            wait(engine, verdict_in)
        verdict_reg = nc.values_load(verdict_i[0:1, 0:1], min_val=0, max_val=3 * Q * P + 4)
        streams = (pe, dve, act, pool)
        counted = [s.n for s in streams]

        with nc.If(verdict_reg == 0):
            def window(s):
                return ps[:, s % RING, 0:KEYS].rearrange("p (t w) -> p t w", w=WINDOW)

            why = "the verdict above: every start is a destination, 0 to N - 1"
            first = {}

            def load_starts(engine, kind, s):
                if s % LOADS == 0:
                    n = min(LOADS, NS - s)
                    first[kind] = nc.values_load_multi_w_load_instructions(
                        starts[:, s:s + n], engines=[kind], min_val=0, max_val=N - 1,
                        skip_runtime_bounds_check_because=why)[1]
                return first[kind][s % LOADS]

            wait(DVE, starts_in, starts_last, *keys_ready)
            wait(ACTE, starts_in, starts_last, *keys_ready)
            wait(PE, *keys_ready)
            dve.mark(DVE.memset(count[:, :, 0:1], 0.0))
            batch_used = {}
            product, written, added = {}, {}, {}

            def one_hot(to, keys, s0, n, width):
                iota = iota2[:, 0:2 * width].rearrange("p (k j) -> p k j", j=2).unsqueeze(1).to_broadcast([P, n, width, 2])
                key = keys.rearrange("p (s j) -> p s j", j=2)[:, s0:s0 + n, :].unsqueeze(2).to_broadcast([P, n, width, 2])
                return dve.mark(DVE.tensor_tensor(to[:, 0:n, :, :], iota, key, ALU.is_equal))

            def add_first(s):
                start = load_starts(DVE, mybir.EngineType.DVE, s)
                wait(DVE, product[s], written[s])
                if s:
                    wait(DVE, added[s - 1])
                column = count[:, :, bass.ds(start, 1)]
                added[s] = dve.mark(DVE.tensor_tensor(column, column, window(s)[:, :, 0:1], ALU.add))

            def write_rest(s):
                start = load_starts(ACTE, mybir.EngineType.Activation, s)
                wait(ACTE, product[s])
                if s:
                    wait(ACTE, written[s - 1])
                to = count[:, :, 1:CW][:, :, bass.ds(start, WINDOW - 1)]
                written[s] = act.mark(ACTE.activation(to, window(s)[:, :, 1:WINDOW], ACT.Copy))

            magnitudes = []
            absw = [agg[:, i, :].rearrange("p (f d) -> p f d", f=HALVES) for i in range(2)]

            def magnitudes_of_weights():
                wait(ACTE, *weights_in, *biases_in, rel_in, act.last)
                for i in range(2):
                    act.mark(ACTE.activation(absw[i], weight[i][:, :, :], ACT.Abs))
                    act.mark(ACTE.activation(scaled[i][:, :], bias[i][:, :], ACT.Abs))
                magnitudes.append(act.mark(ACTE.activation(work[1][REL_ROW:REL_ROW + R, :], work[0][REL_ROW:REL_ROW + R, :],
                                                           ACT.Abs)))

            batches = -(-NS // BATCH)
            besides = norm_x() + [magnitudes_of_weights]
            assert batches > len(besides) + 2
            for b in range(batches + 2):
                s0 = b * BATCH
                n = min(BATCH, NS - s0)
                adds = list(range(max(s0 - 2 * BATCH, 0), min(s0 - BATCH, NS)))
                hot = {}
                made_here = []
                if b < batches:
                    k, half = b % 2, BATCH // 2
                    if s0 % SMALL == 0:
                        g, m = s0 // SMALL, min(SMALL, NS - s0)
                        made_here.append(lambda: one_hot(rel_hot[g % 2], rel_k, s0, m, R))
                        if b == 0:
                            one_hot(rank_hot[0], rank_k, 0, SMALL, WINDOW)
                    elif s0 + BATCH < NS:
                        g, m = (s0 + BATCH) // SMALL, min(SMALL, NS - s0 - BATCH)
                        made_here.append(lambda: one_hot(rank_hot[g % 2], rank_k, s0 + BATCH, m, WINDOW))
                    made_here.append(lambda: one_hot(low_hot[k], low_k, s0, n, P))
                    for i0 in range(0, n, half):
                        made_here.append(lambda i0=i0: hot.update(dict.fromkeys(
                            range(s0 + i0, s0 + i0 + half),
                            one_hot(key_hot[k][:, i0:, :, :], key_k, s0 + i0, min(half, n - i0), KEYS))))
                    if b >= 2:
                        wait(DVE, batch_used[b - 2])
                if b >= 2 and besides:
                    besides.pop(0)()
                while adds or made_here:
                    if made_here and len(made_here) >= len(adds):
                        made_here.pop(0)()
                    if adds:
                        add_first(adds.pop(0))
                    elif made_here:
                        made_here.pop(0)()
                if b < batches:
                    for s in range(s0, s0 + n):
                        i, g = s - s0, s // SMALL
                        wait(PE, hot[s])
                        if s >= RING:
                            wait(PE, written[s - RING], added[s - RING])
                        for j in range(2):
                            PE.matmul(ps[:, s % RING, 0:KEYS], low_hot[b % 2][:, i, :, j], key_hot[b % 2][:, i, :, j],
                                      start=(j == 0), stop=False, skip_group_check=True)
                            last = PE.matmul(ps[REL_ROW:REL_ROW + R, s % RING, (T - 1) * WINDOW:KEYS],
                                             rel_hot[g % 2][:, s % SMALL, :, j], rank_hot[g % 2][:, s % SMALL, :, j],
                                             start=False, stop=(j == 1), skip_group_check=True)
                        product[s] = pe.mark(last)
                        write_rest(s)
                    batch_used[b] = pe.last

            wait(PE, written[NS - 1], added[NS - 1])
            for t in range(T):
                m = rows(t)
                counted_in = pe.mark(PE.matmul(ps[0:m, 0, t:t + 1], count[REL_ROW:REL_ROW + R, T - 1, t * P:t * P + m],
                                               ones16[REL_ROW:REL_ROW + R, :], start=True, stop=True))
            wait(DVE, dve.mark(DVE.memset(newt[:, 3, :], 1.0)), counted_in)
            dve.mark(DVE.tensor_scalar(newt[:, 3, 0:T - 1], ps[:, 0, 0:T - 1], 1.0, None, ALU.add))
            wait(DVE, dve.mark(DVE.tensor_scalar(newt[0:TAIL, 3, T - 1:T], ps[0:TAIL, 0, T - 1:T], 1.0, None, ALU.add)))
            inverse_root(newt[:, 3, :], dinv[:, :], [newt[:, i, :] for i in range(3)])
            wait(DVE, dve.last)

            step_diag = CW + P
            diagonal = flat[:, 0:(T - 1) * step_diag].rearrange("p (t c) -> p t c", c=step_diag)[:, :, 0:P]
            diagonal_tail = count[0:TAIL, T - 1, (T - 1) * P:N]

            def loops(op):
                dve.mark(DVE.tensor_tensor(diagonal, diagonal, ident16[:, :].unsqueeze(1).to_broadcast([P, T - 1, P]), op))
                return dve.mark(DVE.tensor_tensor(diagonal_tail, diagonal_tail, ident16[0:TAIL, 0:TAIL], op))

            SCALE1 = float(2 ** 11)
            dscale_in = dve.mark(DVE.tensor_scalar(dscale[:, :], dinv[:, :], SCALE1, None, ALU.mult))
            wait(DVE, counted_in)
            with_loops = loops(ALU.add)
            wait(ACTE, dscale_in, pe.last)
            table = {}
            for t in range(T):
                m = rows(t)
                high = act.mark(ACTE.activation(node_a[0:m, t, 0, :], h1[0:m, t, :], ACT.Copy, scale=dscale[0:m, t:t + 1]))
                wait(DVE, high)
                table[t] = dve.mark(DVE.scalar_tensor_tensor(
                    out=node_a[0:m, t, 1, :], in0=h1[0:m, t, :], scalar=dscale[0:m, t:t + 1], in1=node_a[0:m, t, 0, :],
                    op0=ALU.mult, op1=ALU.subtract))

            state = {"agg": 0, "w": 0}
            agg_free, w_free = {}, {}
            wait(PE, *magnitudes)
            for i in range(2):
                for f in range(HALVES):
                    summed = pe.mark(PE.matmul(ps[:, 6 + i, 0:D], column_ones, absw[i][:, f, :], start=(f == 0),
                                               stop=(f == HALVES - 1)))
            wait(DVE, summed, act.last)
            for i in range(2):
                w_free[6 + i] = dve.mark(DVE.tensor_reduce(fours[:, i:i + 1], ps[:, 6 + i, 0:D], AX_X, ALU.max))
                dve.mark(DVE.tensor_reduce(fours[:, 2 + i:3 + i], scaled[i][:, :], AX_X, ALU.max))
            relmaxed = dve.mark(DVE.tensor_reduce(bounds[REL_ROW:REL_ROW + R, 7:8], work[1][REL_ROW:REL_ROW + R, :], AX_X, ALU.max))
            wait(POOL, relmaxed)
            reduced = pool.mark(POOL.partition_all_reduce(fours[:, 4:5], bounds[:, 7:8], P, RMAX))
            wait(DVE, dve.last, reduced)
            TOP = 16.0
            wait(DVE, dve.mark(DVE.scalar_tensor_tensor(out=bounds[:, 0:1], in0=fours[:, 0:1], scalar=TOP, in1=fours[:, 2:3],
                                                        op0=ALU.mult, op1=ALU.add)))
            wait(DVE, dve.mark(DVE.scalar_tensor_tensor(out=bounds[:, 1:2], in0=fours[:, 1:2], scalar=bounds[:, 0:1],
                                                        in1=fours[:, 3:4], op0=ALU.mult, op1=ALU.add)))
            dve.mark(DVE.tensor_scalar(bounds[:, 2:3], fours[:, 4:5], TOP, None, ALU.max))
            wait(DVE, dve.last)
            dve.mark(DVE.tensor_scalar(bounds[:, 0:2], bounds[:, 0:2], 1.0, None, ALU.max))
            wait(DVE, dve.last)
            one = 1 << 23
            wait(DVE, dve.mark(DVE.tensor_scalar(bounds[:, 4:7].bitcast(I32), bounds[:, 0:3].bitcast(I32), 0x7F800000, None,
                                                 ALU.bitwise_and)))
            dve.mark(DVE.tensor_scalar(scales[:, 0:3].bitcast(I32), bounds[:, 4:7].bitcast(I32), -1.0, float((2 * 127 + 14) * one),
                                       ALU.mult, ALU.add))
            scales_in = dve.mark(DVE.tensor_scalar(scales[:, 3:6].bitcast(I32), bounds[:, 4:7].bitcast(I32), float(-14 * one), None,
                                                   ALU.add))

            chunks = [0, NC - 1, *range(1, NC - 1)]
            order = [t for c in chunks for t in range(c * CHUNK // P, min((c + 1) * CHUNK // P, T))]

            def sum_edges(nodes, table, c, f, tail_rows, between):
                cols = min(CHUNK, N - c * CHUNK)
                b = state["agg"] % AGG_RING
                state["agg"] += 1
                if b in agg_free:
                    wait(PE, agg_free[b])
                ready_first = [t for t in order if t != T - 1] if c == chunks[0] and f == 0 else range(T - 1)
                for n, t in enumerate([*ready_first, T - 1]):
                    k = P if t < T - 1 else tail_rows
                    if c == chunks[0] and f == 0:
                        wait(PE, table[t])
                    for part in range(2):
                        last = PE.matmul(ps[:, b, 0:cols], nodes[0:k, t, part, f * P:(f + 1) * P],
                                         count[0:k, t, c * CHUNK:c * CHUNK + cols],
                                         start=(n == 0 and part == 0), stop=(n == T - 1 and part == 1))
                    if n == T // 2:
                        between()
                return b, cols, pe.mark(last)

            def evacuate(summed, to, inverse_scale, agg_read):
                b, cols, done = summed
                wait(ACTE, done, *agg_read)
                agg_free[b] = act.mark(ACTE.activation(to[:, 0:cols], ps[:, b, 0:cols], ACT.Copy, scale=inverse_scale))
                return agg_free[b]

            def layer(nodes, table, tail_rows, inverse_scale, steps, sums_in, sums_free=(), at_end=None):
                waiting = []
                read = {k: list(sums_free) for k in range(len(sums_in))}
                spread = len(sums_in) > 1

                def next_step():
                    if waiting:
                        waiting.pop(0)()

                for i, c in enumerate(chunks):
                    halves = []
                    k = i % len(sums_in)
                    for f in range(HALVES):
                        summed = sum_edges(nodes, table, c, f, tail_rows, next_step if spread else lambda: None)
                        if not spread and f == 0 and waiting:
                            while waiting:
                                next_step()
                            read[k] = [pe.last]
                        halves.append(evacuate(summed, sums_in[k][f], inverse_scale, read[k]))
                        if spread:
                            next_step()
                    assert not waiting
                    if spread and i:
                        read[1 - k] = [pe.last]
                    waiting = steps(c, sums_in[k], halves)
                if at_end:
                    at_end()
                while waiting:
                    next_step()

            def by_tile(tile):
                def steps(c, sums, halves):
                    return [lambda t=t: tile(t, t * P - c * CHUNK, halves) for t in order if t * P // CHUNK == c]
                return steps

            one_buffer = [[agg[:, f, :] for f in range(HALVES)]]

            def conv_tile(i, t, at_col, halves, w_in):
                m = rows(t)
                b = 4 + state["w"] % 4
                state["w"] += 1
                if b in w_free:
                    wait(PE, w_free[b])
                wait(PE, *halves, w_in)
                for f in range(HALVES):
                    done = PE.matmul(ps[0:m, b, 0:D], agg[:, f, at_col:at_col + m], weight[i % 2][:, f, :], start=(f == 0),
                                     stop=(f == HALVES - 1))
                return b, pe.mark(done)

            work_free = {0: None, 1: None}

            def relu_layer(i, nodes, table, nodes_next, inverse_scale):
                wait(DVE, act.last, dve.last)
                wait(DVE, dve.mark(DVE.tensor_scalar(dscale[:, :], dinv[:, :], scales[:, i:i + 1], None, ALU.mult)))
                new = {}

                def tile(t, at_col, halves):
                    m, k = rows(t), t % 2
                    b, done = conv_tile(i, t, at_col, halves, weights_in[i])
                    wait(DVE, done, dve.last)
                    w_free[b] = dve.mark(DVE.scalar_tensor_tensor(
                        out=work[k][0:m, :], in0=ps[0:m, b, 0:D], scalar=dinv[0:m, t:t + 1], in1=bias[i][0:m, :],
                        op0=ALU.mult, op1=ALU.add))
                    wait(DVE, w_free[b], *([work_free[k]] if work_free[k] else []))
                    ready = dve.mark(DVE.tensor_scalar(scaled[k][0:m, :], work[k][0:m, :], 0.0, dscale[0:m, t:t + 1],
                                                       ALU.max, ALU.mult))
                    wait(ACTE, ready)
                    high = act.mark(ACTE.activation(nodes_next[0:m, t, 0, :], scaled[k][0:m, :], ACT.Copy))
                    wait(DVE, high)
                    new[t] = dve.mark(DVE.tensor_tensor(nodes_next[0:m, t, 1, :], scaled[k][0:m, :],
                                                        nodes_next[0:m, t, 0, :], ALU.subtract))
                    work_free[k] = new[t]

                layer(nodes, table, TAIL, inverse_scale, by_tile(tile), one_buffer)
                return new

            wait(ACTE, scales_in)
            table2 = relu_layer(0, node_a, table, node_b, 1.0 / SCALE1)
            wait(SP, pe.last)
            weights_in.append(dma("w2_in", SP, weight[0][:, :, :], convs[2][0].rearrange("(f p) d -> p f d", p=P)))
            table3 = relu_layer(1, node_b, table2, node_a, scales[:, 3:4])

            wait(DVE, pe.last, rel_in, scales_in)
            wait(ACTE, dve.mark(DVE.memset(node_b[:, T - 1, :, :], 0.0)))
            relation = slice(REL_ROW, REL_ROW + R)
            rel_again = dma("rel_again", SP, xt[0][relation, :], relvec)
            wait(ACTE, rel_again)
            high = act.mark(ACTE.activation(node_b[relation, T - 1, 0, :], xt[0][relation, :], ACT.Copy, scale=scales[relation, 2:3]))
            wait(DVE, high)
            rel_table = dve.mark(DVE.scalar_tensor_tensor(
                out=node_b[relation, T - 1, 1, :], in0=xt[0][relation, :], scalar=scales[relation, 2:3],
                in1=node_b[relation, T - 1, 0, :], op0=ALU.mult, op1=ALU.subtract))
            wait(SP, rel_table)

            x_tile = [xt[0][:, :], xt[1][:, :], weight[1][:, 0, :], weight[1][:, 1, :]]
            x_loads = [stream(f"x_again{k}", 16) for k in range(len(x_tile))]
            x1_stores = [stream(f"x1_out{k}", 16) for k in range(len(x_tile))]
            x_here, x1_read = {}, {}
            table4 = {}
            order_of = {t: i for i, t in enumerate(order)}

            def load_x(i):
                t, k = order[i], i % len(x_tile)
                wait(SP, *x1_read.get(i - len(x_tile), []))
                x_here[t] = x_loads[k].mark(SP.dma_start(x_tile[k][0:rows(t), :], x[t * P:t * P + rows(t), :]))

            def norm_steps(c, sums, halves):
                tiles = [t for t in order if t * P // CHUNK == c]
                first, end = tiles[0], tiles[-1] + 1
                cols = slice(first, end)
                x1 = {t: x_tile[order_of[t] % len(x_tile)][0:rows(t), :] for t in tiles}

                def step():
                    stored = {}
                    done, x1_here, stats_here = {}, {}, {}
                    for t in tiles:
                        done[t] = conv_tile(2, t, t * P - c * CHUNK, halves, weights_in[2])
                    wait(DVE, dve.last, act.last)
                    for t in tiles:
                        m, k = rows(t), t % 2
                        b, product_here = done[t]
                        wait(DVE, product_here)
                        w_free[b] = dve.mark(DVE.scalar_tensor_tensor(
                            out=work[k][0:m, :], in0=ps[0:m, b, 0:D], scalar=dinv[0:m, t:t + 1], in1=bias[2][0:m, :],
                            op0=ALU.mult, op1=ALU.add))
                        wait(DVE, w_free[b], x_here[t])
                        x1_here[t] = dve.mark(DVE.tensor_tensor(x1[t], x1[t], work[k][0:m, :], ALU.add))
                        wait(SP, x1_here[t])
                        stored[t] = x1_stores[order_of[t] % len(x_tile)].mark(
                            SP.dma_start(x1_dram[t * P:t * P + m, :], x1[t]))
                        wait(DVE, x1_here[t])
                        wait(DVE, dve.mark(DVE.bn_stats(stats[0:m, k, :], x1[t])))
                        wait(DVE, dve.mark(DVE.bn_aggr(moments[0:m, t, :], stats[0:m, k, :])))
                    wait(DVE, dve.mark(DVE.tensor_scalar(newt[:, 3, cols], moments[:, cols, 1], EPS, None, ALU.add)))
                    inverse_root(newt[:, 3, cols], rstd[:, cols], [newt[:, i, cols] for i in range(3)])
                    wait(DVE, dve.last)
                    wait(DVE, dve.mark(DVE.scalar_tensor_tensor(out=negmr[:, cols], in0=moments[:, cols, 0], scalar=-1.0,
                                                                in1=rstd[:, cols], op0=ALU.mult, op1=ALU.mult)))
                    for n, of in enumerate((rstd, negmr)):
                        ready = dve.mark(DVE.tensor_scalar(newt[:, n, cols], of[:, cols], scales[:, 2:3], None, ALU.mult))
                    wait(ACTE, ready)
                    for t in tiles:
                        m, k = rows(t), t % 2
                        if work_free[k]:
                            wait(ACTE, work_free[k])
                        shaped = act.mark(ACTE.activation(scaled[k][0:m, :], x1[t], ACT.Relu,
                                                          bias=newt[0:m, 1, t:t + 1], scale=newt[0:m, 0, t:t + 1]))
                        x1_read[order_of[t]] = [shaped, stored[t]]
                        wait(ACTE, shaped)
                        high = act.mark(ACTE.activation(node_b[0:m, t, 0, :], scaled[k][0:m, :], ACT.Copy))
                        wait(DVE, high)
                        table4[t] = dve.mark(DVE.tensor_tensor(node_b[0:m, t, 1, :], scaled[k][0:m, :],
                                                               node_b[0:m, t, 0, :], ALU.subtract))
                        work_free[k] = table4[t]
                    for t in tiles:
                        if order_of[t] + len(x_tile) < T:
                            load_x(order_of[t] + len(x_tile))
                return [step]

            for i in range(len(x_tile)):
                load_x(i)

            def take_loops_out():
                wait(DVE, pe.last)
                loops_out.append(loops(ALU.subtract))

            loops_out = []
            layer(node_a, table3, TAIL, scales[:, 4:5], norm_steps, one_buffer, at_end=take_loops_out)

            wait(PE, *loops_out)
            gru = gru_setup("", [s.last for s in x1_stores], order)

            def gru_step(t, at_col, sums, halves):
                gru(order_of[t], [sums[f][:, at_col:at_col + rows(t)] for f in range(HALVES)], halves)

            def gru_steps(c, sums, halves):
                return [lambda t=t: gru_step(t, t * P - c * CHUNK, sums, halves) for t in order if t * P // CHUNK == c]

            two_buffers = one_buffer + [[weight[f][:, :, :].rearrange("p f d -> p (f d)") for f in range(HALVES)]]
            layer(node_b, table4, REL_ROW + R, scales[:, 5:6], gru_steps, two_buffers, [pe.last, dve.last])

        for s, n in zip(streams, counted):
            s.n = n

        with nc.Else():
            def settle(*engines, also=()):
                for engine in engines:
                    wait(engine, pe.last, dve.last, act.last, *also)

            at[0] = 0
            node_iota = early(N)
            hot = early(N)
            sums = early(HALVES * N).rearrange("p (f n) -> p f n", f=HALVES)
            message = early(D)
            relation_row = early(D)
            source_id, target_id, relation_id = (early(1, I32) for _ in range(3))
            ones_g, zeros_g = early(P), early(BANK)
            node_iota_i = hot.bitcast(I32)
            a32, b32 = (n[:, :, :, :].rearrange("p t a d -> p (t a d)").bitcast(F32).rearrange("p (t d) -> p t d", t=T)
                        for n in (node_a, node_b))
            for step in norm_x():
                step()
            settle(POOL, DVE, also=[pool.last, rel_in, *biases_in, *weights_in[:2]])
            numbered = pool.mark(POOL.iota(node_iota_i, pattern=[[1, N]], base=0, channel_multiplier=0))
            wait(DVE, numbered)
            dve.mark(DVE.tensor_copy(node_iota, node_iota_i))
            dve.mark(DVE.memset(ones_g, 1.0))
            dve.mark(DVE.memset(zeros_g, 0.0))
            settle(DVE, PE)

            def handoff(name):
                return ctx.enter_context(nc.semaphore(name))

            def take(engine, sem, n):
                engine.wait_ge(sem, n)
                engine.sem_inc(sem, -n)

            source_here, target_here, relation_here = handoff("source_here"), handoff("target_here"), handoff("relation_here")
            gathered = {}
            hot_here, block_done = handoff("hot_here"), handoff("block_done")
            EDGE_BLOCKS, EDGES_LEFT = E // P, E % P

            def banks():
                return [(c, c * BANK, min(BANK, N - c * BANK)) for c in range(-(-N // BANK))]

            def each_edge_block(products, table=None, relations=False):
                message_here, relation_row_here = gathered.get("now", (None, None))

                def block(k, ids, i):
                    SP.dma_start(target_id[0:k, :], ids(dst)).then_inc(target_here, 16)
                    take(DVE, target_here, 16)
                    DVE.tensor_scalar(hot[0:k, :], node_iota[0:k, :], target_id[0:k, :], None, ALU.is_equal).then_inc(hot_here, 1)
                    if table is not None:
                        SP.dma_start(source_id[0:k, :], ids(src)).then_inc(source_here, 16)
                        take(POOL, source_here, 16)
                        POOL.indirect_dma_start(out=message[0:k, :], out_offset=None, in_=table,
                                                in_offset=bass.IndirectOffsetOnAxis(ap=source_id[0:k, 0:1], axis=0)
                                                ).then_inc(message_here.sem, 16)
                        PE.wait_ge(message_here.sem, i * 16 + (message_here.n + 16))
                    if relations:
                        SP.dma_start(relation_id[0:k, :], ids(rel)).then_inc(relation_here, 16)
                        take(POOL, relation_here, 16)
                        POOL.indirect_dma_start(out=relation_row[0:k, :], out_offset=None, in_=relvec,
                                                in_offset=bass.IndirectOffsetOnAxis(ap=relation_id[0:k, 0:1], axis=0)
                                                ).then_inc(relation_row_here.sem, 16)
                        PE.wait_ge(relation_row_here.sem, i * 16 + (relation_row_here.n + 16))
                    take(PE, hot_here, 1)
                    products(k).then_inc(block_done, 1)
                    take(SP, block_done, 1)

                with nc.Fori(0, EDGE_BLOCKS) as i:
                    block(P, lambda v: v[0:EDGE_BLOCKS * P].rearrange("(b p) -> b p", p=P)[bass.ds(i, 1), :]
                          .rearrange("b p -> p b"), i)
                if EDGES_LEFT:
                    block(EDGES_LEFT, lambda v: v[EDGE_BLOCKS * P:E].rearrange("(p b) -> p b", b=1), EDGE_BLOCKS)
                blocks = EDGE_BLOCKS + (EDGES_LEFT > 0)
                if table is not None:
                    message_here.n += 16 * blocks
                if relations:
                    relation_row_here.n += 16 * blocks

            def clear(bank, cols):
                return pe.mark(PE.matmul(ps[:, bank, 0:cols], zeros_g[:, 0:P], zeros_g[:, 0:cols], start=True, stop=False,
                                         skip_group_check=True))

            clear(0, T)

            def count_block(k):
                for t in range(T):
                    m = rows(t)
                    last = PE.matmul(ps[0:m, 0, t:t + 1], hot[0:k, t * P:t * P + m], ones_g[0:k, 0:1], start=False,
                                     stop=False, skip_group_check=True)
                return last

            each_edge_block(count_block)
            pe.mark(PE.matmul(ps[:, 0, 0:T], zeros_g[:, 0:P], zeros_g[:, 0:T], start=False, stop=True, skip_group_check=True))
            settle(DVE)
            dve.mark(DVE.tensor_scalar(newt[:, 3, :], ps[:, 0, 0:T], 1.0, None, ALU.add))
            wait(DVE, dve.last)
            inverse_root(newt[:, 3, :], dinv[:, :], [newt[:, i, :] for i in range(3)])
            settle(DVE, ACTE)
            for t in range(T):
                dve.mark(DVE.tensor_scalar(b32[0:rows(t), t, :], b32[0:rows(t), t, :], dinv[0:rows(t), t:t + 1], None,
                                           ALU.mult))
            table_out = stream("table_out", 16)

            def sum_all(nodes, loops, relations):
                gathered["now"] = stream(f"message_here{table_out.n}", 16), stream(f"relation_row_here{table_out.n}", 16)
                settle(SP, also=[table_out.last])
                table_out.mark(SP.dma_start(table_dram[0:(T - 1) * P, :].rearrange("(t p) d -> p t d", p=P),
                                            nodes[:, 0:T - 1, :]))
                table_out.mark(SP.dma_start(table_dram[(T - 1) * P:N, :], nodes[0:TAIL, T - 1, :]))
                wait(POOL, table_out.last)
                for f in range(HALVES):
                    settle(PE, also=[table_out.last])
                    for c, _, cols in banks():
                        clear(c, cols)
                    settle(DVE)

                    def sum_block(k):
                        for rows_of in (message, relation_row)[:2 if relations else 1]:
                            for c, start, cols in banks():
                                last = PE.matmul(ps[:, c, 0:cols], rows_of[0:k, f * P:(f + 1) * P], hot[0:k, start:start + cols],
                                                 start=False, stop=False, skip_group_check=True)
                        return last

                    each_edge_block(sum_block, table_dram, relations)
                    if loops:
                        for t in range(T):
                            m, c = rows(t), t * P // BANK
                            PE.matmul(ps[:, c, t * P - c * BANK:t * P - c * BANK + m], nodes[0:m, t, f * P:(f + 1) * P],
                                      ident[0:m, 0:m], start=False, stop=False, skip_group_check=True)
                    for c, _, cols in banks():
                        pe.mark(PE.matmul(ps[:, c, 0:cols], zeros_g[:, 0:P], zeros_g[:, 0:cols], start=False, stop=True,
                                          skip_group_check=True))
                    settle(DVE)
                    for c, start, cols in banks():
                        dve.mark(DVE.tensor_copy(sums[:, f, start:start + cols], ps[:, c, 0:cols]))

            def product_tile(t, w):
                settle(PE)
                for f in range(HALVES):
                    last = PE.matmul(ps[0:rows(t), 7, 0:D], sums[:, f, t * P:t * P + rows(t)], w[:, f, :], start=(f == 0),
                                     stop=(f == HALVES - 1))
                return pe.mark(last)

            for i, (nodes, following) in enumerate(((b32, a32), (a32, b32))):
                sum_all(nodes, True, False)
                for t in range(T):
                    m, k = rows(t), t % 2
                    product_tile(t, weight[i])
                    settle(DVE)
                    wait(DVE, dve.mark(DVE.scalar_tensor_tensor(
                        out=work[k][0:m, :], in0=ps[0:m, 7, 0:D], scalar=dinv[0:m, t:t + 1], in1=bias[i][0:m, :],
                        op0=ALU.mult, op1=ALU.add)))
                    dve.mark(DVE.tensor_scalar(following[0:m, t, :], work[k][0:m, :], 0.0, dinv[0:m, t:t + 1],
                                               ALU.max, ALU.mult))
            sum_all(b32, True, False)
            settle(SP)
            w3_here = dma("w2_in_g", SP, weight[0][:, :, :], convs[2][0].rearrange("(f p) d -> p f d", p=P))
            wait(PE, w3_here)
            streams_g = [stream(f"x_again_g{k}", 16) for k in range(2)], [stream(f"x1_out_g{k}", 16) for k in range(2)]
            x_read_g = {}
            for t in range(T):
                m, k = rows(t), t % 2
                done = product_tile(t, weight[0])
                settle(SP)
                residual_tile(t, 7, done, streams_g, x_read_g)
                settle(ACTE)
                act.mark(ACTE.activation(a32[0:m, t, :], xt[k][0:m, :], ACT.Relu, bias=negmr[0:m, t:t + 1],
                                         scale=rstd[0:m, t:t + 1]))
                x_read_g[k].append(act.last)
            sum_all(a32, False, True)
            gru_g = gru_setup("g_", [s.last for s in streams_g[1]] + [table_out.last], range(T))
            for t in range(T):
                settle(PE)
                gru_g(t, [sums[:, f, t * P:t * P + rows(t)] for f in range(HALVES)], [])


_INPUTS = ("x", "src", "dst", "edge_type_16", "L0_gnn_W1", "L0_gnn_b1", "L0_gnn_W2", "L0_gnn_b2", "L0_gnn_W3",
           "L0_gnn_b3", "L1_gnn_relvectors", "L1_gnn_w_ih", "L1_gnn_w_hh", "L1_gnn_b_ih", "L1_gnn_b_hh")


def kernel(**inputs):
    import numpy as np
    import concourse.bacc as bacc
    from concourse import mybir as mb
    from concourse.bass_utils import run_bass_kernel_spmd

    nc = bacc.Bacc("TRN2", target_bir_lowering=False, num_devices=1, dynamic_dma_scratch_size=1024)
    arrays, ap = {}, {}
    for name in _INPUTS:
        a = np.asarray(inputs[name])
        if name in ("L1_gnn_w_ih", "L1_gnn_w_hh"):
            a = a.T
        a = np.ascontiguousarray(a)
        arrays[f"in_{name}"] = a
        ap[name] = nc.dram_tensor(f"in_{name}", a.shape, mb.dt.from_np(a.dtype), kind="ExternalInput").ap()
    shape = tuple(arrays["in_x"].shape)
    out = nc.dram_tensor("out_0", shape, mb.dt.float32, kind="ExternalOutput").ap()
    x1 = nc.dram_tensor("x1_scratch", shape, mb.dt.float32, kind="Internal").ap()
    table = nc.dram_tensor("table_scratch", shape, mb.dt.float32, kind="Internal").ap()
    convs = [(ap[f"L0_gnn_W{i}"], ap[f"L0_gnn_b{i}"]) for i in (1, 2, 3)]
    program(nc, ap["x"], ap["src"], ap["dst"], ap["edge_type_16"], convs, ap["L1_gnn_relvectors"], ap["L1_gnn_w_ih"],
            ap["L1_gnn_w_hh"], ap["L1_gnn_b_ih"], ap["L1_gnn_b_hh"], x1, table, out)
    result = run_bass_kernel_spmd(nc, [arrays], core_ids=[0])
    return result.results[0]["out_0"]
```

```python
from contextlib import ExitStack

import concourse.bass as bass
from concourse import mybir

ALU = mybir.AluOpType
ACT = mybir.ActivationFunctionType
AX_X = mybir.AxisListType.X
F32, F16, I32 = mybir.dt.float32, mybir.dt.float16, mybir.dt.int32
RADD = bass.bass_isa.ReduceOp.add
RMAX = bass.bass_isa.ReduceOp.max

P = 128
EPS = 1e-5
BANK = 512
SUPER = 2 * P
WINDOW = 11
BATCH = 4
SMALL = 8
REL_ROW = 64
RING = 6
EARLY = 5
FIRST_EARLY = 118
AGG_RING = 3
LOADS = 16


class Stream:

    def __init__(self, ctx, nc, name, by=1):
        self.sem, self.by, self.n = ctx.enter_context(nc.semaphore(name)), by, 0

    def mark(self, instruction):
        instruction.then_inc(self.sem, self.by)
        self.n += self.by
        return self.sem, self.n

    @property
    def last(self):
        return self.sem, self.n


def wait(engine, *marks):
    for sem, value in marks:
        engine.wait_ge(sem, value)


def program(nc, x, src, dst, rel, convs, relvec, w_ih_t, w_hh_t, b_ih, b_hh, x1_dram, table_dram, out):
    N, D = x.shape
    E = src.shape[0]
    R = relvec.shape[0]
    T = -(-N // P)
    TAIL = N - (T - 1) * P
    NS = -(-E // SUPER)
    Q = -(-NS // P)
    FULL = E // SUPER
    LEFT = E - FULL * SUPER
    KEYS = T * WINDOW
    CW = (N + WINDOW) // 2 * 2
    HALVES = D // P
    G = 3 * D
    CHUNK = BANK
    NC = -(-N // CHUNK)
    assert BATCH < RING < 2 * BATCH and D == 2 * P and FULL == NS - 1 and 2 * LEFT >= SUPER and TAIL <= REL_ROW - 11 and R <= 16 and NS > 7
    SP, PE, DVE, ACTE, POOL = nc.sync, nc.tensor, nc.vector, nc.scalar, nc.gpsimd

    def rows(t):
        return P if t < T - 1 else TAIL

    with ExitStack() as ctx:
        def sb(name, shape, dt):
            return ctx.enter_context(nc.sbuf_tensor(name, shape, dt))

        def stream(name, by=1):
            return Stream(ctx, nc, name, by)

        count = sb("count", [P, T, CW], F16)
        node_a = sb("node_a", [P, T, 2, D], F16)
        node_b = sb("node_b", [P, T, 2, D], F16)
        weight = [sb(f"weight{i}", [P, HALVES, D], F32) for i in range(2)]
        bias = [sb(f"bias{i}", [P, D], F32) for i in range(3)]
        agg = sb("agg", [P, HALVES, CHUNK], F32)
        work = [sb(f"work{i}", [P, D], F32) for i in range(2)]
        scaled = [sb(f"scaled{i}", [P, D], F32) for i in range(2)]
        xt = [sb(f"xt{i}", [P, D], F32) for i in range(2)]
        ident = sb("ident", [P, P], F32)
        ident16 = sb("ident16", [P, P], F16)
        ones16 = sb("ones16", [P, 1], F16)
        stats = sb("stats", [P, 2, 6], F32)
        moments = sb("moments", [P, T, 2], F32)
        rstd = sb("rstd", [P, T], F32)
        negmr = sb("negmr", [P, T], F32)
        dinv = sb("dinv", [P, T], F32)
        dscale = sb("dscale", [P, T], F32)
        newt = sb("newt", [P, 4, T], F32)
        fours = sb("fours", [P, 8], F32)
        bounds = sb("bounds", [P, 8], F32)
        scales = sb("scales", [P, 8], F32)
        verdict = sb("verdict", [P, 1], F32)
        verdict_i = sb("verdict_i", [1, 1], I32)

        flat = count[:, :, :].rearrange("p t c -> p (t c)")
        at = [0]

        def early(n, dt=F32):
            words = flat[:, at[0]:at[0] + 2 * n]
            at[0] += 2 * n
            return words.bitcast(dt)

        src_row, dst_row, rel_row, high_row, low_row = (
            early(Q * SUPER, I32).rearrange("p (q e) -> p q e", q=Q) for _ in range(5))
        low_r, key_r, rel_r, rank_r = (early(Q * SUPER // 2).bitcast(F16).rearrange("p (q e) -> p q e", q=Q)
                                       for _ in range(4))
        next_row = early(Q, I32)
        chain = early(NS + 1)
        ones = early(P)
        iota_i = early(2 * KEYS, I32)
        start_f = early(NS + 1)
        rules = early(2 * Q + 3 * Q + 4 + EARLY)
        assert at[0] <= T * CW

        ASIDE = CW // 2 - CW // 2 % 2 - 68

        def aside(t, n, first=0):
            return count[:, t, ASIDE + first:ASIDE + first + n]

        assert ASIDE > 128 * (WINDOW - 1) and ASIDE + 4 * NS <= CW
        rank_is = [aside(6 + w // 2, 2 * NS, 2 * NS * (w % 2)) for w in range(WINDOW)]
        low_of = [aside(12 + q, WINDOW * P).rearrange("p (w k) -> p w k", w=WINDOW) for q in range(Q)]
        high_of = aside(16, WINDOW * Q * T).rearrange("p (w q k) -> p w q k", w=WINDOW, q=Q)
        first_node = aside(17, 2 * Q, 4).bitcast(I32)
        steps_w, node_i, low_i, high_i = (
            aside(17, 2 * WINDOW * Q, 100 + 2 * WINDOW * Q * i).bitcast(I32).rearrange("p (w q) -> p w q", w=WINDOW)
            for i in range(4))
        low_h, high_h = (aside(18, WINDOW * Q, WINDOW * Q * i).rearrange("p (w q) -> p w q", w=WINDOW) for i in range(2))
        degree = aside(19, 8 * T).bitcast(F32).rearrange("p (i t) -> p i t", i=4)

        h1 = node_a[:, :, :, :].rearrange("p t a d -> p (t a d)").bitcast(F32).rearrange("p (t d) -> p t d", t=T)

        flat_a, flat_b = (n[:, :, :, :].rearrange("p t a d -> p (t a d)") for n in (node_a, node_b))
        at_a = [0]

        def piece(of, n, dt=F16):
            size = n if dt == F16 else 2 * n
            words = of[:, at_a[0]:at_a[0] + size]
            at_a[0] += size
            return words if dt == F16 else words.bitcast(dt)

        def while_counting(n, dt=F16):
            return piece(flat_b, n, dt)

        iota2 = while_counting(2 * KEYS)
        low_k, key_k, rel_k, rank_k = (while_counting(2 * NS) for _ in range(4))
        starts = while_counting(NS + 1, I32)[0:1, :]
        key_hot = [while_counting(BATCH * KEYS * 2).rearrange("p (s k j) -> p s k j", s=BATCH, j=2) for _ in range(2)]
        low_hot = [while_counting(BATCH * P * 2).rearrange("p (s k j) -> p s k j", s=BATCH, j=2) for _ in range(2)]
        rel_hot = [while_counting(SMALL * R * 2).rearrange("p (s k j) -> p s k j", s=SMALL, j=2) for _ in range(2)]
        rank_hot = [while_counting(SMALL * WINDOW * 2).rearrange("p (s k j) -> p s k j", s=SMALL, j=2)
                    for _ in range(2)]
        assert at_a[0] <= T * 2 * D

        ps = ctx.enter_context(nc.psum_tensor("ps", [P, 8, BANK], F32))

        pe, dve, act, pool = stream("pe_done"), stream("dve_done"), stream("act_done"), stream("pool_done")

        def dma(name, engine, to, of, **kw):
            return stream(name, 16).mark(engine.dma_start(to, of, **kw))

        whole = (Q - 1) * P
        rest = FULL - whole
        pads = []
        pads.append(dve.mark(DVE.memset(src_row[:, Q - 1, :], -1)))
        pads.append(dve.mark(DVE.memset(dst_row[:, Q - 1, :], -1)))
        pads.append(dve.mark(DVE.memset(rel_row[:, Q - 1, :], -1)))
        pads.append(dve.mark(DVE.memset(next_row[:, :], N)))
        starts_in = dma("starts", ACTE, starts[:, 0:FULL],
                        dst[0:FULL * SUPER].rearrange("(p s e) -> p s e", p=1, e=SUPER)[:, :, 0],
                        allow_slow_non_contiguous=True)
        starts_last = dma("starts_last", ACTE, starts[:, FULL:NS],
                          dst[FULL * SUPER:FULL * SUPER + 1].rearrange("(p e) -> p e", p=1))
        wait(ACTE, dve.last)
        nexts = [dma("next_full", ACTE, next_row[:, 0:Q - 1],
                     dst[SUPER:(whole + 1) * SUPER].rearrange("(q p e) -> p q e", p=P, e=SUPER)[:, :, 0],
                     allow_slow_non_contiguous=True),
                 dma("next_rest", ACTE, next_row[0:rest, Q - 1:Q],
                     dst[whole * SUPER + 1:FULL * SUPER + 1].rearrange("(p e) -> p e", e=SUPER)[:, SUPER - 1:SUPER],
                     allow_slow_non_contiguous=True)]
        edges_in = {}
        for name, row, of in (("src", src_row, src), ("dst", dst_row, dst), ("rel", rel_row, rel)):
            edges_in[name] = [dma(f"{name}_full", SP, row[:, 0:Q - 1, :],
                                  of[0:whole * SUPER].rearrange("(q p e) -> p q e", p=P, e=SUPER))]
            wait(SP, dve.last)
            edges_in[name].append(dma(f"{name}_rest", SP, row[0:rest, Q - 1, :],
                                      of[whole * SUPER:FULL * SUPER].rearrange("(p e) -> p e", e=SUPER)))
            edges_in[name].append(dma(f"{name}_left", SP, row[rest:rest + 1, Q - 1, 0:LEFT],
                                      of[FULL * SUPER:E].rearrange("(p e) -> p e", p=1)))
        edges_in["dst"].append(dma("dst_pad", SP, dst_row[rest:rest + 1, Q - 1, LEFT:SUPER],
                                   dst[E - (SUPER - LEFT):E].rearrange("(p e) -> p e", p=1)))
        wait(SP, *edges_in["rel"])
        assert (T - 1) % 6 == 0
        x_in = [dma(f"x_in{g}", SP, h1[:, g * 6:g * 6 + 6, :],
                    x[g * 6 * P:(g * 6 + 6) * P, :].rearrange("(t p) d -> p t d", p=P)) for g in range((T - 1) // 6)]
        x_tail = dma("x_tail", SP, h1[0:TAIL, T - 1, :], x[(T - 1) * P:N, :])
        weights_in = [dma(f"w{i}_in", SP, weight[i][:, :, :], convs[i][0].rearrange("(f p) d -> p f d", p=P))
                      for i in range(2)]
        biases_in = [dma(f"b{i}_in", SP, bias[i][:, :],
                         convs[i][1].rearrange("(p d) -> p d", p=1).to_broadcast([P, D])) for i in range(3)]
        rel_in = dma("rel_in", SP, work[0][REL_ROW:REL_ROW + R, :], relvec)

        made = pool.mark(POOL.iota(iota_i[:, :], pattern=[[1, KEYS], [0, 2]], base=0, channel_multiplier=0))
        made_w = pool.mark(POOL.iota(steps_w, pattern=[[1, WINDOW], [0, Q]], base=0, channel_multiplier=0))
        wait(DVE, made)
        dve.mark(DVE.tensor_copy(iota2[:, :], iota_i[:, :]))
        ident_zero = dve.mark(DVE.memset(ident[:, :], 0.0))
        dve.mark(DVE.memset(ones[:, :], 1.0))
        dve.mark(DVE.memset(ones16[:, :], 1.0))
        dve.mark(DVE.memset(bounds[:, :], 0.0))
        dve.mark(DVE.memset(rules, 0.0))
        dve.mark(DVE.memset(moments[:, :, :], 1.0))
        dve.mark(DVE.memset(newt[:, :, :], 1.0))
        column_ones = xt[0][:, 0:P]
        dve.mark(DVE.memset(column_ones, 1.0))
        wait(POOL, ident_zero)
        ident_in = pool.mark(POOL.affine_select(out=ident[:, :], in_=ident[:, :], compare_op=ALU.not_equal, fill=1.0,
                                                base=0, pattern=[[-1, P]], channel_multiplier=1))
        wait(DVE, ident_in)
        ident16_in = dve.mark(DVE.tensor_copy(ident16[:, :], ident[:, :]))

        row_max, row_min = rules[:, 0:Q], rules[:, Q:2 * Q]
        broken_rows = rules[:, 2 * Q:5 * Q].rearrange("p (r q) -> p r q", q=Q)
        broken_all = rules[:, 5 * Q:5 * Q + 4 + EARLY]
        gap = 7
        wait(DVE, starts_in, starts_last)
        wait(DVE, dve.mark(DVE.tensor_copy(start_f[0:1, 0:NS], starts[:, 0:NS])))
        wait(DVE, dve.mark(DVE.tensor_tensor(chain[0:1, 0:NS - 1], start_f[0:1, 1:NS], start_f[0:1, 0:NS - 1], ALU.subtract)))
        wait(DVE, dve.mark(DVE.tensor_reduce(broken_all[0:1, 0:1], chain[0:1, 0:NS - 1], AX_X, ALU.max)))
        wait(DVE, dve.mark(DVE.tensor_tensor(chain[0:1, 0:NS - gap], start_f[0:1, gap:NS], start_f[0:1, 0:NS - gap], ALU.subtract)))
        wait(DVE, dve.mark(DVE.tensor_reduce(broken_all[0:1, 1:2], chain[0:1, 0:NS - gap], AX_X, ALU.min)))
        dve.mark(DVE.tensor_scalar(broken_all[0:1, 0:1], broken_all[0:1, 0:1], float(WINDOW - 1), None, ALU.is_gt))
        dve.mark(DVE.tensor_scalar(broken_all[0:1, 1:2], broken_all[0:1, 1:2], 1.0, None, ALU.is_lt))
        dve.mark(DVE.tensor_scalar(broken_all[0:1, 2:3], start_f[0:1, 0:1], 0.0, None, ALU.is_gt))
        dve.mark(DVE.tensor_scalar(broken_all[0:1, 3:4], start_f[0:1, NS - 1:NS], float(N - WINDOW), None, ALU.is_lt))

        def settled(c):
            return -(-(c + 1) * CHUNK * FULL // N) + 3 + c

        for c in range(EARLY):
            dve.mark(DVE.tensor_scalar(broken_all[0:1, 4 + c:5 + c], start_f[0:1, settled(c):settled(c) + 1],
                                       float((c + 1) * CHUNK), None, ALU.is_lt))

        wait(DVE, *edges_in["src"])
        low_here = dve.mark(DVE.tensor_scalar(low_row, src_row, P - 1, None, ALU.bitwise_and))
        dve.mark(DVE.tensor_scalar(high_row, src_row, 7, None, ALU.arith_shift_right))
        wait(DVE, *edges_in["dst"])
        rank_done = dve.mark(DVE.tensor_tensor(rank_r, dst_row, dst_row[:, :, 0:1].to_broadcast([P, Q, SUPER]), ALU.subtract))
        wait(DVE, rank_done)
        key_done = dve.mark(DVE.scalar_tensor_tensor(out=key_r, in0=high_row, scalar=float(WINDOW), in1=rank_r,
                                                     op0=ALU.mult, op1=ALU.add))
        dve.mark(DVE.tensor_copy(first_node, dst_row[:, :, 0]))
        wait(ACTE, low_here)
        low_done = act.mark(ACTE.activation(low_r, low_row, ACT.Copy))
        wait(ACTE, *edges_in["rel"])
        rel_done = act.mark(ACTE.activation(rel_r, rel_row, ACT.Copy))

        dve.mark(DVE.tensor_reduce(row_max, dst_row, AX_X, ALU.max))
        dve.mark(DVE.tensor_reduce(row_min, dst_row, AX_X, ALU.min))
        wait(DVE, *nexts, dve.last)
        dve.mark(DVE.tensor_tensor(broken_rows[:, 0, :], row_max, dst_row[:, :, 0], ALU.subtract))
        dve.mark(DVE.tensor_tensor(broken_rows[:, 1, :], row_min, dst_row[:, :, 0], ALU.subtract))
        dve.mark(DVE.tensor_tensor(broken_rows[:, 2, :], row_max, next_row, ALU.subtract))
        wait(DVE, dve.last)
        dve.mark(DVE.tensor_scalar(broken_rows[:, 0, :], broken_rows[:, 0, :], float(WINDOW - 1), None, ALU.is_gt))
        dve.mark(DVE.tensor_scalar(broken_rows[:, 1, :], broken_rows[:, 1, :], 0.0, None, ALU.is_lt))
        dve.mark(DVE.tensor_scalar(broken_rows[:, 2, :], broken_rows[:, 2, :], 0.0, None, ALU.is_gt))
        wait(DVE, dve.last)
        broken = dve.mark(DVE.tensor_reduce(verdict[:, :], rules[:, 2 * Q:5 * Q + 4 + EARLY], AX_X, ALU.add))

        turned = []
        for bank, (row, ready) in enumerate(((low_r, low_done), (rel_r, rel_done), (rank_r, rank_done), (key_r, key_done))):
            wait(PE, ready, ident16_in)
            half_bank = ps[:, bank, :].bitcast(F16).rearrange("p (j s) -> p j s", j=2)
            for j in range(2):
                for q in range(Q):
                    last = PE.transpose(half_bank[:, j, q * P:(q + 1) * P], row[:, q, j * P:(j + 1) * P], ident16[:, :])
            turned.append((half_bank[:, :, 0:NS], pe.mark(last)))
        for (transposed, ready), k in zip(turned, (low_k, rel_k, rank_k, key_k)):
            wait(ACTE, ready)
            act.mark(ACTE.activation(k.rearrange("p (s j) -> p j s", j=2), transposed, ACT.Copy))
        wait(PE, broken)
        judged = pe.mark(PE.matmul(ps[0:1, 4, 0:1], verdict[:, :], ones[:, 0:1], start=True, stop=True))
        wait(DVE, judged)
        verdict_in = dve.mark(DVE.tensor_copy(verdict_i[:, :], ps[0:1, 4, 0:1]))
        keys_ready = [act.last, dve.last]

        def root_steps(src_ap, dst_ap, tmp):
            done = []

            def root():
                wait(ACTE, dve.last)
                done.append(act.mark(ACTE.activation(tmp[0], src_ap, ACT.Sqrt)))

            def on_dve(instruction):
                def step():
                    wait(DVE, done[-1])
                    done.append(dve.mark(instruction()))
                return step

            return [root,
                    on_dve(lambda: DVE.reciprocal(tmp[1], tmp[0])),
                    on_dve(lambda: DVE.tensor_tensor(tmp[2], tmp[1], tmp[1], ALU.mult)),
                    on_dve(lambda: DVE.tensor_tensor(tmp[2], tmp[2], src_ap, ALU.mult)),
                    on_dve(lambda: DVE.tensor_scalar(tmp[2], tmp[2], -0.5, 1.5, ALU.mult, ALU.add)),
                    on_dve(lambda: DVE.tensor_tensor(dst_ap, tmp[1], tmp[2], ALU.mult))]

        def inverse_root(src_ap, dst_ap, tmp):
            for step in root_steps(src_ap, dst_ap, tmp):
                step()
            wait(DVE, dve.last)

        def norm_x():
            used, ready = [None, None], {}

            def x_tile_of(t):
                return h1[0:rows(t), t, :]

            def total(t):
                m, k = rows(t), t % 2
                wait(ACTE, x_in[t // 6] if t < T - 1 else x_tail)
                if used[k]:
                    wait(ACTE, used[k])
                used[k] = act.mark(ACTE.activation(scaled[k][0:m, :], x_tile_of(t), ACT.Copy,
                                                   accum_out=newt[0:m, 0, t:t + 1]))

            def mean():
                wait(DVE, *used)
                ready["mean"] = dve.mark(DVE.tensor_scalar(negmr[:, :], newt[:, 0, :], -1.0 / D, None, ALU.mult))

            def squares(t):
                m, k = rows(t), t % 2
                wait(ACTE, used[k], ready["mean"])
                used[k] = act.mark(ACTE.activation(scaled[k][0:m, :], x_tile_of(t), ACT.Square, bias=negmr[0:m, t:t + 1],
                                                   accum_out=newt[0:m, 2, t:t + 1]))

            def variance():
                wait(DVE, *used)
                dve.mark(DVE.tensor_scalar(newt[:, 3, :], newt[:, 2, :], 1.0 / D, EPS, ALU.mult, ALU.add))

            def mean_over_deviation():
                wait(DVE, dve.last)
                ready["norm"] = dve.mark(DVE.tensor_tensor(negmr[:, :], negmr[:, :], rstd[:, :], ALU.mult))

            return ([lambda t=t: total(t) for t in range(T)], mean, [lambda t=t: squares(t) for t in range(T)],
                    [variance, *root_steps(newt[:, 3, :], rstd[:, :], [newt[:, i, :] for i in range(3)]),
                     mean_over_deviation])

        def residual_tile(t, b, done, streams, x_read):
            m, k = rows(t), t % 2
            x_loads, x1_stores = streams
            if k in x_read:
                wait(SP, *x_read[k])
            x_here = x_loads[k].mark(SP.dma_start(xt[k][0:m, :], x[t * P:t * P + m, :]))
            wait(DVE, done, dve.last)
            product_read = dve.mark(DVE.scalar_tensor_tensor(
                out=work[k][0:m, :], in0=ps[0:m, b, 0:D], scalar=dinv[0:m, t:t + 1], in1=bias[2][0:m, :],
                op0=ALU.mult, op1=ALU.add))
            wait(DVE, product_read, x_here)
            x1_here = dve.mark(DVE.tensor_tensor(xt[k][0:m, :], xt[k][0:m, :], work[k][0:m, :], ALU.add))
            wait(ACTE, x1_here)
            stored = x1_stores[k].mark(ACTE.dma_start(x1_dram[t * P:t * P + m, :], xt[k][0:m, :]))
            wait(DVE, x1_here)
            wait(DVE, dve.mark(DVE.bn_stats(stats[0:m, k, :], xt[k][0:m, :])))
            wait(DVE, dve.mark(DVE.bn_aggr(moments[0:m, t, :], stats[0:m, k, :])))
            wait(DVE, dve.mark(DVE.tensor_scalar(newt[0:m, 3, t:t + 1], moments[0:m, t, 1:2], EPS, None, ALU.add)))
            inverse_root(newt[0:m, 3, t:t + 1], rstd[0:m, t:t + 1], [newt[0:m, i, t:t + 1] for i in range(3)])
            wait(DVE, dve.last)
            dve.mark(DVE.scalar_tensor_tensor(out=negmr[0:m, t:t + 1], in0=moments[0:m, t, 0:1], scalar=-1.0,
                                              in1=rstd[0:m, t:t + 1], op0=ALU.mult, op1=ALU.mult))
            x_read[k] = [dve.last, stored]
            return product_read

        def gru_setup(tag, x1_stored, order):
            at_a[0] = 0
            w_ih_sb, w_hh_sb = (piece(flat_a, HALVES * G, F32).rearrange("p (f g) -> p f g", f=HALVES) for _ in range(2))
            bias_rz, bias_rz2 = piece(flat_a, 2 * D, F32), piece(flat_a, 2 * D, F32)
            bias_in, bias_hn = piece(flat_a, D, F32), piece(flat_a, D, F32)
            h_t = [piece(flat_a, HALVES * P, F32).rearrange("p (f n) -> p f n", f=HALVES) for _ in range(2)]
            gate_rz = [piece(flat_a, 2 * D, F32), bias_rz2]
            x1_tile = [xt[0][:, :], xt[1][:, :], piece(flat_a, D, F32)]
            h_tile = [scaled[0][:, :], scaled[1][:, :], piece(flat_a, D, F32)]
            n_tile = work
            AHEAD = len(x1_tile)
            assert at_a[0] <= T * 2 * D
            wait(SP, pe.last, dve.last, act.last, *x1_stored)
            x1_loads = [stream(tag + f"x1_in{k}", 16) for k in range(AHEAD)]
            out_stores = [stream(tag + f"out{k}", 16) for k in range(AHEAD)]

            def load_x1(i):
                t = order[i]
                return x1_loads[i % AHEAD].mark(SP.dma_start(x1_tile[i % AHEAD][0:rows(t), :],
                                                             x1_dram[t * P:t * P + rows(t), :]))

            x1_here = {i: load_x1(i) for i in range(AHEAD)}
            w_gru_in = [dma(tag + "w_ih_in", SP, w_ih_sb, w_ih_t.rearrange("(f p) g -> p f g", p=P)),
                        dma(tag + "w_hh_in", SP, w_hh_sb, w_hh_t.rearrange("(f p) g -> p f g", p=P))]

            def spread(v):
                return v.rearrange("(p d) -> p d", p=1).to_broadcast([P, v.shape[0]])

            b_gru_in = [dma(tag + "b_rz_in", SP, bias_rz, spread(b_ih[0:2 * D])), dma(tag + "b_rz2_in", SP, bias_rz2, spread(b_hh[0:2 * D])),
                        dma(tag + "b_in_in", SP, bias_in, spread(b_ih[2 * D:G])), dma(tag + "b_hn_in", SP, bias_hn, spread(b_hh[2 * D:G]))]
            norms_here = dve.last
            H_BANK, RZ_BANK, N_BANK = 3, (4, 5), (6, 7)
            h_here, h_turned, n_done, n_sum, z_read, result, kept = {}, {}, {}, {}, {}, {}, {}
            bias_here = []

            def make_h(i):
                t, k = order[i], i % AHEAD
                m = rows(t)
                wait(ACTE, x1_here[i], norms_here)
                if i >= AHEAD:
                    wait(ACTE, kept[i - AHEAD])
                h_here[i] = act.mark(ACTE.activation(h_tile[k][0:m, :], x1_tile[k][0:m, :], ACT.Relu,
                                                     bias=negmr[0:m, t:t + 1], scale=rstd[0:m, t:t + 1]))

            def turn_h(i):
                m = rows(order[i])
                wait(PE, h_here[i])
                if i:
                    wait(PE, h_turned[i - 1])
                for f in range(HALVES):
                    turned = pe.mark(PE.transpose(ps[:, H_BANK, f * P:f * P + m], h_tile[i % AHEAD][0:m, f * P:(f + 1) * P],
                                                  ident[0:m, 0:m]))
                wait(ACTE, turned)
                if i >= 2:
                    wait(ACTE, n_done[i - 2])
                h_turned[i] = act.mark(ACTE.activation(
                    h_t[i % 2][:, :, 0:m], ps[:, H_BANK, 0:HALVES * P].rearrange("p (f n) -> p f n", f=HALVES)[:, :, 0:m], ACT.Copy))

            def gru_tile(i, sums, halves):
                t, k, x = order[i], i % 2, i % AHEAD
                m = rows(t)
                if i == 0:
                    make_h(0)
                    turn_h(0)
                    wait(DVE, *b_gru_in)
                    bias_here.append(dve.mark(DVE.tensor_tensor(bias_rz, bias_rz, bias_rz2, ALU.add)))
                if i + 1 < T:
                    make_h(i + 1)
                rz, nn = RZ_BANK[k], N_BANK[k]
                wait(PE, *halves, *w_gru_in, h_turned[i])
                if i >= 2:
                    wait(PE, n_sum[i - 2])
                hs = [h_t[k][:, f, 0:m] for f in range(HALVES)]
                for n, (l, w, f) in enumerate([(sums[f], w_ih_sb, f) for f in range(HALVES)] +
                                              [(hs[f], w_hh_sb, f) for f in range(HALVES)]):
                    done = PE.matmul(ps[0:m, rz, 0:2 * D], l, w[:, f, 0:2 * D], start=(n == 0), stop=(n == 2 * HALVES - 1))
                rz_done = pe.mark(done)
                for col, ls, w in ((0, sums, w_ih_sb), (D, hs, w_hh_sb)):
                    for f in range(HALVES):
                        done = PE.matmul(ps[0:m, nn, col:col + D], ls[f], w[:, f, 2 * D:G], start=(f == 0),
                                         stop=(f == HALVES - 1))
                n_done[i] = pe.mark(done)
                if i + 1 < T:
                    turn_h(i + 1)
                rz_gate, v, h = gate_rz[k], n_tile[k][0:m, :], h_tile[x][0:m, :]
                wait(DVE, rz_done, *bias_here)
                if i >= 2:
                    wait(DVE, z_read[i - 2], result[i - 2])
                biased = dve.mark(DVE.tensor_tensor(rz_gate[0:m, :], ps[0:m, rz, :], bias_rz[0:m, :], ALU.add))
                wait(ACTE, biased)
                gates = act.mark(ACTE.activation(rz_gate[0:m, :], rz_gate[0:m, :], ACT.Sigmoid))
                wait(DVE, n_done[i])
                wait(DVE, dve.mark(DVE.tensor_tensor(v, ps[0:m, nn, D:2 * D], bias_hn[0:m, :], ALU.add)), gates)
                wait(DVE, dve.mark(DVE.tensor_tensor(v, v, rz_gate[0:m, 0:D], ALU.mult)))
                n_sum[i] = dve.mark(DVE.tensor_tensor(v, ps[0:m, nn, 0:D], v, ALU.add))
                wait(DVE, n_sum[i])
                wait(ACTE, dve.mark(DVE.tensor_tensor(v, v, bias_in[0:m, :], ALU.add)))
                new_n = act.mark(ACTE.activation(v, v, ACT.Tanh))
                wait(DVE, new_n)
                wait(DVE, dve.mark(DVE.tensor_tensor(h, h, v, ALU.subtract)))
                z_read[i] = dve.mark(DVE.tensor_tensor(h, h, rz_gate[0:m, D:2 * D], ALU.mult))
                dve.mark(DVE.tensor_tensor(v, v, x1_tile[x][0:m, :], ALU.add))
                wait(DVE, dve.last)
                result[i] = dve.mark(DVE.tensor_tensor(h, h, v, ALU.add))
                wait(SP, result[i])
                kept[i] = out_stores[x].mark(SP.dma_start(out[t * P:t * P + m, :], h))
                if i + AHEAD < T:
                    x1_here[i + AHEAD] = load_x1(i + AHEAD)
                if i == T - 1:
                    wait(SP, *[s.last for s in out_stores])
            return gru_tile

        for engine in (SP, PE, DVE, ACTE, POOL):
            wait(engine, verdict_in)
        verdict_reg = nc.values_load(verdict_i[0:1, 0:1], min_val=0, max_val=3 * Q * P + 4 + EARLY)
        streams = (pe, dve, act, pool)
        counted = [s.n for s in streams]

        with nc.If(verdict_reg == 0):
            def window(s):
                return ps[:, s % RING, 0:KEYS].rearrange("p (t w) -> p t w", w=WINDOW)

            why = "the verdict above: every start is a destination, 0 to N - 1"
            first = {}

            def load_starts(engine, kind, s):
                if s % LOADS == 0:
                    n = min(LOADS, NS - s)
                    first[kind] = nc.values_load_multi_w_load_instructions(
                        starts[:, s:s + n], engines=[kind], min_val=0, max_val=N - 1,
                        skip_runtime_bounds_check_because=why)[1]
                return first[kind][s % LOADS]

            wait(DVE, starts_in, starts_last, *keys_ready)
            wait(ACTE, starts_in, starts_last, *keys_ready)
            wait(PE, *keys_ready)
            dve.mark(DVE.memset(count[:, :, 0:1], 0.0))
            batch_used = {}
            product, written, added = {}, {}, {}

            def one_hot(to, keys, s0, n, width):
                iota = iota2[:, 0:2 * width].rearrange("p (k j) -> p k j", j=2).unsqueeze(1).to_broadcast([P, n, width, 2])
                key = keys.rearrange("p (s j) -> p s j", j=2)[:, s0:s0 + n, :].unsqueeze(2).to_broadcast([P, n, width, 2])
                return dve.mark(DVE.tensor_tensor(to[:, 0:n, :, :], iota, key, ALU.is_equal))

            def add_first(s):
                start = load_starts(DVE, mybir.EngineType.DVE, s)
                wait(DVE, product[s], written[s])
                if s:
                    wait(DVE, added[s - 1])
                column = count[:, :, bass.ds(start, 1)]
                added[s] = dve.mark(DVE.tensor_tensor(column, column, window(s)[:, :, 0:1], ALU.add))

            def write_rest(s):
                start = load_starts(ACTE, mybir.EngineType.Activation, s)
                wait(ACTE, product[s])
                if s:
                    wait(ACTE, written[s - 1])
                to = count[:, :, 1:CW][:, :, bass.ds(start, WINDOW - 1)]
                written[s] = act.mark(ACTE.activation(to, window(s)[:, :, 1:WINDOW], ACT.Copy))

            SCALE1 = float(2 ** 11)
            step_diag = CW + P

            def loops(op, first=0, end=T):
                full = min(end, T - 1)
                start = first * step_diag
                diagonal = flat[:, start:start + (full - first) * step_diag].rearrange("p (t c) -> p t c", c=step_diag)[:, :, 0:P]
                done = dve.mark(DVE.tensor_tensor(diagonal, diagonal,
                                                  ident16[:, :].unsqueeze(1).to_broadcast([P, full - first, P]), op))
                if end == T:
                    tail = count[0:TAIL, T - 1, (T - 1) * P:N]
                    done = dve.mark(DVE.tensor_tensor(tail, tail, ident16[0:TAIL, 0:TAIL], op))
                return done

            beside = {}

            def at_superblock(s, step):
                beside.setdefault(s, []).append(step)

            def lanes(q):
                return min(P, NS - q * P)

            CNT, HIST = ps[:, 6, 0:WINDOW * Q], ps[:, 7, 0:T]
            seen = {}

            def rank_is_step(w):
                seen[w] = dve.mark(DVE.tensor_scalar(rank_is[w], rank_k, float(w), None, ALU.is_equal))

            def count_step(w):
                wait(PE, seen[w], seen["clear"])
                for q in range(Q):
                    for j in range(2):
                        last = PE.matmul(ps[0:lanes(q), 6, w * Q + q:w * Q + q + 1],
                                         rank_is[w].rearrange("p (s j) -> p s j", j=2)[:, q * P:q * P + lanes(q), j],
                                         ones16[:, :], start=(j == 0), stop=(j == 1))
                seen["counts"] = pe.mark(last)

            def nodes_step():
                wait(DVE, made_w)
                wait(DVE, dve.mark(DVE.tensor_tensor(node_i, steps_w, first_node.unsqueeze(1).to_broadcast([P, WINDOW, Q]), ALU.add)))
                dve.mark(DVE.tensor_scalar(low_i, node_i, P - 1, None, ALU.bitwise_and))
                wait(DVE, dve.mark(DVE.tensor_scalar(high_i, node_i, 7, None, ALU.arith_shift_right)))
                dve.mark(DVE.tensor_copy(low_h, low_i))
                seen["nodes"] = dve.mark(DVE.tensor_copy(high_h, high_i))

            def tile_numbers(n):
                return iota2.rearrange("p (k j) -> p k j", j=2)[:, 0:n, 0]

            def low_of_step(q):
                wait(DVE, seen["nodes"])
                dve.mark(DVE.tensor_tensor(low_of[q], tile_numbers(P).unsqueeze(1).to_broadcast([P, WINDOW, P]),
                                           low_h[:, :, q].unsqueeze(2).to_broadcast([P, WINDOW, P]), ALU.is_equal))

            high_flat = high_of.rearrange("p w q k -> p (w q) k")

            def high_of_step():
                wait(DVE, seen["nodes"])
                seen["high"] = dve.mark(DVE.tensor_tensor(
                    high_flat, tile_numbers(T).unsqueeze(1).to_broadcast([P, WINDOW * Q, T]),
                    high_h.rearrange("p w q -> p (w q)").unsqueeze(2).to_broadcast([P, WINDOW * Q, T]), ALU.is_equal))

            def times_counts_step():
                wait(DVE, seen["counts"], seen["high"])
                seen["weighted"] = dve.mark(DVE.tensor_tensor(high_flat, high_flat,
                                                              CNT.unsqueeze(2).to_broadcast([P, WINDOW * Q, T]), ALU.mult))

            def histogram_step():
                wait(PE, seen["weighted"])
                for w in range(WINDOW):
                    for q in range(Q):
                        last = PE.matmul(HIST, low_of[q][0:lanes(q), w, :], high_of[0:lanes(q), w, q, :],
                                         start=(w == 0 and q == 0), stop=(w == WINDOW - 1 and q == Q - 1))
                seen["degrees"] = pe.mark(last)

            def degree_step():
                wait(DVE, seen["degrees"])
                dve.mark(DVE.tensor_scalar(degree[:, 3, :], HIST, 1.0, None, ALU.add))

            spare = [agg[:, f, h * D:(h + 1) * D] for f in range(HALVES) for h in range(2)] + [n[:, :] for n in scaled]
            table, shaped, turned_high = {}, {}, {}

            def table_factors():
                wait(DVE, dve.last)
                wait(DVE, dve.mark(DVE.tensor_scalar(dscale[:, :], dinv[:, :], SCALE1, None, ALU.mult)))
                dve.mark(DVE.tensor_tensor(newt[:, 0, :], rstd[:, :], dscale[:, :], ALU.mult))
                seen["factors"] = dve.mark(DVE.tensor_tensor(newt[:, 1, :], negmr[:, :], dscale[:, :], ALU.mult))

            def shape_step(t):
                m = rows(t)
                wait(ACTE, seen["factors"])
                if t >= len(spare):
                    wait(ACTE, table[t - len(spare)])
                elif t >= 4:
                    wait(ACTE, seen["squares"])
                shaped[t] = act.mark(ACTE.activation(spare[t % len(spare)][0:m, :], h1[0:m, t, :], ACT.Relu,
                                                     bias=newt[0:m, 1, t:t + 1], scale=newt[0:m, 0, t:t + 1]))

            def high_step(t):
                m = rows(t)
                wait(ACTE, shaped[t])
                turned_high[t] = act.mark(ACTE.activation(node_a[0:m, t, 0, :], spare[t % len(spare)][0:m, :], ACT.Copy))

            def low_step(t):
                m = rows(t)
                wait(DVE, turned_high[t])
                table[t] = dve.mark(DVE.tensor_tensor(node_a[0:m, t, 1, :], spare[t % len(spare)][0:m, :],
                                                      node_a[0:m, t, 0, :], ALU.subtract))

            behind = 2 * BATCH
            totals, mean, squares, factors = norm_x()

            final = slice(2 * (NS - 1), 2 * NS)
            padding = aside(17, 2)
            wait(DVE, dve.mark(DVE.tensor_scalar(padding, rel_k[:, final], 0.0, 64.0, ALU.is_lt, ALU.mult)))
            wait(DVE, dve.mark(DVE.tensor_tensor(rank_k[:, final], rank_k[:, final], padding, ALU.add)))

            def clear_step():
                seen["clear"] = dve.mark(DVE.memset(CNT, 0.0))

            at_superblock(0, clear_step)
            for w in range(WINDOW):
                at_superblock(w, lambda w=w: rank_is_step(w))
                at_superblock(w + 2, lambda w=w: count_step(w))
            at_superblock(WINDOW, nodes_step)
            for q in range(Q):
                at_superblock(WINDOW + 1 + q, lambda q=q: low_of_step(q))
            at_superblock(WINDOW + 1 + Q, high_of_step)
            at_superblock(WINDOW + 2 + Q + behind, times_counts_step)
            at_superblock(WINDOW + 3 + Q + behind, histogram_step)
            s = WINDOW + 3 + Q + 2 * behind
            at_superblock(s, degree_step)
            for i, step in enumerate(root_steps(degree[:, 3, :], dinv[:, :], [degree[:, i, :] for i in range(3)])):
                at_superblock(s + (behind + i if i else 0), step)
            for t in range(T):
                at_superblock(t, totals[t])
            s = T + behind
            at_superblock(s, mean)
            for t in range(T):
                at_superblock(s + 1 + t, squares[t])
            s += T + behind
            at_superblock(s, lambda: seen.update(squares=act.last))
            at_superblock(s, factors[0])
            at_superblock(s, factors[1])
            for i, step in enumerate([*factors[2:], table_factors]):
                at_superblock(s + behind + i, step)
            s += behind + len(factors)
            for t in range(T):
                at_superblock(s + 2 * t, lambda t=t: shape_step(t))
                at_superblock(s + 2 * t + 1, lambda t=t: high_step(t))
                at_superblock(s + 2 * t + behind + 3, lambda t=t: low_step(t))

            early_out = [stream(f"early_out{f}", 16) for f in range(HALVES)]
            flat_dram = table_dram.rearrange("n d -> (n d)")

            def early_dram(c):
                size = P * HALVES * CHUNK
                return flat_dram[c * size:(c + 1) * size].rearrange("(p f k) -> p f k", f=HALVES, k=CHUNK)

            looped, early_free = {}, {}

            def early_loops(c):
                wait(DVE, written[settled(c) - 1], added[settled(c) - 1])
                looped[c] = loops(ALU.add, c * CHUNK // P, (c + 1) * CHUNK // P)

            last_early = settled(EARLY - 1) + behind
            for c in range(EARLY):
                at_superblock(settled(c) + behind, lambda c=c: early_loops(c))
                assert settled(c) + behind < FIRST_EARLY + c * (last_early - FIRST_EARLY) / (EARLY - 1) + 1

            def products_due(s):
                chunk = 2 * HALVES * T
                if s < last_early:
                    return (s - FIRST_EARLY + 1) * (EARLY - 1) * chunk / (last_early - FIRST_EARLY)
                return (EARLY - 1 + (s - last_early + 1) / (NS - 1 - last_early)) * chunk

            def early_products():
                for c in range(EARLY):
                    wait(PE, looped[c], written[settled(c) - 1], added[settled(c) - 1])
                    for f in range(HALVES):
                        if c:
                            wait(PE, early_free[f])
                        for t in range(T):
                            k = rows(t)
                            if c == 0 and f == 0:
                                wait(PE, table[t], *([seen["degrees"], degrees_read[0]] if t == 0 else []))
                            for part in range(2):
                                last = PE.matmul(ps[:, 6 + f, :], node_a[0:k, t, part, f * P:(f + 1) * P],
                                                 count[0:k, t, c * CHUNK:(c + 1) * CHUNK],
                                                 start=(t == 0 and part == 0), stop=(t == T - 1 and part == 1))
                                if t == T - 1 and part == 1:
                                    summed = pe.mark(last)
                                    wait(ACTE, summed, *([early_out[f].last] if c else [table[T - 1]]))
                                    early_free[f] = act.mark(ACTE.activation(agg[:, f, :], ps[:, 6 + f, :], ACT.Copy,
                                                                             scale=1.0 / SCALE1))
                                    wait(SP, early_free[f])
                                    early_out[f].mark(SP.dma_start(early_dram(c)[:, f, :], agg[:, f, :]))
                                yield

            products = early_products()
            issued = 0
            degrees_read = []
            at_superblock(FIRST_EARLY - 1, lambda: degrees_read.append(dve.last))

            batches = -(-NS // BATCH)
            for b in range(batches + 2):
                s0 = b * BATCH
                n = min(BATCH, NS - s0)
                adds = list(range(max(s0 - RING, 0), min(s0 - RING + BATCH, NS)))
                hot = {}
                made_here = []
                if b < batches:
                    k, half = b % 2, BATCH // 2
                    if s0 % SMALL == 0:
                        g, m = s0 // SMALL, min(SMALL, NS - s0)
                        made_here.append(lambda: one_hot(rel_hot[g % 2], rel_k, s0, m, R))
                        if b == 0:
                            one_hot(rank_hot[0], rank_k, 0, SMALL, WINDOW)
                    elif s0 + BATCH < NS:
                        g, m = (s0 + BATCH) // SMALL, min(SMALL, NS - s0 - BATCH)
                        made_here.append(lambda: one_hot(rank_hot[g % 2], rank_k, s0 + BATCH, m, WINDOW))
                    made_here.append(lambda: one_hot(low_hot[k], low_k, s0, n, P))
                    for i0 in range(0, n, half):
                        made_here.append(lambda i0=i0: hot.update(dict.fromkeys(
                            range(s0 + i0, s0 + i0 + half),
                            one_hot(key_hot[k][:, i0:, :, :], key_k, s0 + i0, min(half, n - i0), KEYS))))
                    if b >= 2:
                        wait(DVE, batch_used[b - 2])
                while adds or made_here:
                    if made_here and len(made_here) >= len(adds):
                        made_here.pop(0)()
                    if adds:
                        add_first(adds.pop(0))
                    elif made_here:
                        made_here.pop(0)()
                if b < batches:
                    for s in range(s0, s0 + n):
                        i, g = s - s0, s // SMALL
                        wait(PE, hot[s])
                        if s >= RING:
                            wait(PE, written[s - RING], added[s - RING])
                        for j in range(2):
                            PE.matmul(ps[:, s % RING, 0:KEYS], low_hot[b % 2][:, i, :, j], key_hot[b % 2][:, i, :, j],
                                      start=(j == 0), stop=False, skip_group_check=True)
                            last = PE.matmul(ps[REL_ROW:REL_ROW + R, s % RING, (T - 1) * WINDOW:KEYS],
                                             rel_hot[g % 2][:, s % SMALL, :, j], rank_hot[g % 2][:, s % SMALL, :, j],
                                             start=False, stop=(j == 1), skip_group_check=True)
                        product[s] = pe.mark(last)
                        batch_used[b] = pe.last
                        write_rest(s)
                        for step in beside.pop(s, []):
                            step()
                        while s >= FIRST_EARLY and issued < products_due(s):
                            next(products, None)
                            issued += 1
            assert not beside and next(products, "over") == "over"

            wait(PE, written[NS - 1], added[NS - 1])
            wait(DVE, written[NS - 1], added[NS - 1])
            with_loops = loops(ALU.add, EARLY * CHUNK // P)
            wait(SP, pe.last, written[NS - 1], added[NS - 1], *[o.last for o in early_out])
            early_here = {c: dma(f"early_in{c}", SP,
                                 flat_b[:, c * 2 * HALVES * CHUNK:(c + 1) * 2 * HALVES * CHUNK].bitcast(F32)
                                 .rearrange("p (f k) -> p f k", f=HALVES), early_dram(c)) for c in range(EARLY)}
            wait(PE, with_loops)

            state = {"agg": 0, "w": 0}
            agg_free, w_free = {}, {}
            def scale_step():
                absw = [agg[:, i, :].rearrange("p (f d) -> p f d", f=HALVES) for i in range(2)]
                wait(ACTE, *weights_in, *biases_in, rel_in, *[o.last for o in early_out])
                for i in range(2):
                    act.mark(ACTE.activation(absw[i], weight[i][:, :, :], ACT.Abs))
                    act.mark(ACTE.activation(scaled[i][:, :], bias[i][:, :], ACT.Abs))
                wait(PE, act.mark(ACTE.activation(work[1][REL_ROW:REL_ROW + R, :], work[0][REL_ROW:REL_ROW + R, :], ACT.Abs)))
                for i in range(2):
                    for f in range(HALVES):
                        summed = pe.mark(PE.matmul(ps[:, 6 + i, 0:D], column_ones, absw[i][:, f, :], start=(f == 0),
                                                   stop=(f == HALVES - 1)))
                wait(DVE, summed)
                for i in range(2):
                    w_free[6 + i] = dve.mark(DVE.tensor_reduce(fours[:, i:i + 1], ps[:, 6 + i, 0:D], AX_X, ALU.max))
                    dve.mark(DVE.tensor_reduce(fours[:, 2 + i:3 + i], scaled[i][:, :], AX_X, ALU.max))
                relmaxed = dve.mark(DVE.tensor_reduce(bounds[REL_ROW:REL_ROW + R, 7:8], work[1][REL_ROW:REL_ROW + R, :], AX_X, ALU.max))
                wait(POOL, relmaxed)
                reduced = pool.mark(POOL.partition_all_reduce(fours[:, 4:5], bounds[:, 7:8], P, RMAX))
                wait(DVE, dve.last, reduced)
                TOP = 16.0
                wait(DVE, dve.mark(DVE.scalar_tensor_tensor(out=bounds[:, 0:1], in0=fours[:, 0:1], scalar=TOP, in1=fours[:, 2:3],
                                                            op0=ALU.mult, op1=ALU.add)))
                wait(DVE, dve.mark(DVE.scalar_tensor_tensor(out=bounds[:, 1:2], in0=fours[:, 1:2], scalar=bounds[:, 0:1],
                                                            in1=fours[:, 3:4], op0=ALU.mult, op1=ALU.add)))
                dve.mark(DVE.tensor_scalar(bounds[:, 2:3], fours[:, 4:5], TOP, None, ALU.max))
                wait(DVE, dve.last)
                dve.mark(DVE.tensor_scalar(bounds[:, 0:2], bounds[:, 0:2], 1.0, None, ALU.max))
                wait(DVE, dve.last)
                one = 1 << 23
                wait(DVE, dve.mark(DVE.tensor_scalar(bounds[:, 4:7].bitcast(I32), bounds[:, 0:3].bitcast(I32), 0x7F800000, None,
                                                     ALU.bitwise_and)))
                dve.mark(DVE.tensor_scalar(scales[:, 0:3].bitcast(I32), bounds[:, 4:7].bitcast(I32), -1.0, float((2 * 127 + 14) * one),
                                           ALU.mult, ALU.add))
                scales_in = dve.mark(DVE.tensor_scalar(scales[:, 3:6].bitcast(I32), bounds[:, 4:7].bitcast(I32), float(-14 * one), None,
                                                       ALU.add))
                seen["scales"] = scales_in
                return scales_in

            chunks = [0, NC - 1, *range(1, NC - 1)]
            order = [t for c in chunks for t in range(c * CHUNK // P, min((c + 1) * CHUNK // P, T))]

            def sum_edges(nodes, table, c, f, tail_rows, between):
                cols = min(CHUNK, N - c * CHUNK)
                b = state["agg"] % AGG_RING
                state["agg"] += 1
                if b in agg_free:
                    wait(PE, agg_free[b])
                ready_first = [t for t in order if t != T - 1] if c == chunks[0] and f == 0 else range(T - 1)
                for n, t in enumerate([*ready_first, T - 1]):
                    k = P if t < T - 1 else tail_rows
                    if c == chunks[0] and f == 0:
                        wait(PE, table[t])
                    for part in range(2):
                        last = PE.matmul(ps[:, b, 0:cols], nodes[0:k, t, part, f * P:(f + 1) * P],
                                         count[0:k, t, c * CHUNK:c * CHUNK + cols],
                                         start=(n == 0 and part == 0), stop=(n == T - 1 and part == 1))
                    if n == T - 1:
                        done = pe.mark(last)
                    between(n)
                return b, cols, done

            def evacuate(summed, to, inverse_scale, agg_read):
                b, cols, done = summed
                wait(ACTE, done, *agg_read)
                agg_free[b] = act.mark(ACTE.activation(to[:, 0:cols], ps[:, b, 0:cols], ACT.Copy, scale=inverse_scale))
                return agg_free[b]

            def first_layer(nodes, table, inverse_scale, early_steps, steps, start_steps):
                waiting, left = list(early_steps), []

                def between(i, f, n):
                    if i == 0 and f == 0 and n == T // 2:
                        start_steps()
                    elif n in (T // 4, T // 2, 3 * T // 4, T - 1) and (i or f or n > T // 2) and waiting:
                        waiting.pop(0)()

                for i, c in enumerate(range(EARLY, NC)):
                    halves = []
                    for f in range(HALVES):
                        summed = sum_edges(nodes, table, c, f, TAIL, lambda n: between(i, f, n))
                        if f == 0:
                            while left:
                                left.pop(0)()
                        halves.append(evacuate(summed, agg[:, f, :], inverse_scale, [pe.last]))
                    left = steps(c, agg, halves)
                while waiting or left:
                    (waiting or left).pop(0)()

            def layer(nodes, table, tail_rows, inverse_scale, steps, sums_in, sums_free=(), at_end=None):
                waiting = []
                read = {k: list(sums_free) for k in range(len(sums_in))}
                spread = len(sums_in) > 1

                def next_step():
                    if waiting:
                        waiting.pop(0)()

                for i, c in enumerate(chunks):
                    halves = []
                    k = i % len(sums_in)
                    for f in range(HALVES):
                        summed = sum_edges(nodes, table, c, f, tail_rows, (lambda n: next_step() if n == T // 2 else None) if spread else lambda n: None)
                        if not spread and f == 0 and waiting:
                            while waiting:
                                next_step()
                            read[k] = [pe.last]
                        halves.append(evacuate(summed, sums_in[k][f], inverse_scale, read[k]))
                        if spread:
                            next_step()
                    assert not waiting
                    if spread and i:
                        read[1 - k] = [pe.last]
                    waiting = steps(c, sums_in[k], halves)
                if at_end:
                    at_end()
                while waiting:
                    next_step()

            def by_tile(tile, flush):
                def steps(c, sums, halves):
                    return [*[lambda t=t: tile(t, t * P - c * CHUNK, halves) for t in order if t * P // CHUNK == c], flush]
                return steps

            one_buffer = [[agg[:, f, :] for f in range(HALVES)]]

            def conv_tile(i, t, at_col, halves, w_in, sums=agg):
                m = rows(t)
                b = 4 + state["w"] % 4
                state["w"] += 1
                if b in w_free:
                    wait(PE, w_free[b])
                wait(PE, *halves, w_in)
                for f in range(HALVES):
                    done = PE.matmul(ps[0:m, b, 0:D], sums[:, f, at_col:at_col + m], weight[i % 2][:, f, :], start=(f == 0),
                                     stop=(f == HALVES - 1))
                return b, pe.mark(done)

            work_free = {0: None, 1: None}

            def relu_tiles(i, nodes_next, new):
                def start():
                    wait(DVE, act.last, dve.last)
                    wait(DVE, dve.mark(DVE.tensor_scalar(dscale[:, :], dinv[:, :], scales[:, i:i + 1], None, ALU.mult)))

                def tile(t, at_col, halves):
                    finish(t, *conv_tile(i, t, at_col, halves, weights_in[i]))

                lows, shaped = [], {}

                def finish(t, b, done):
                    m, k = rows(t), t % 2
                    wait(DVE, done, *shaped.get(k, []))
                    w_free[b] = dve.mark(DVE.scalar_tensor_tensor(
                        out=work[k][0:m, :], in0=ps[0:m, b, 0:D], scalar=dinv[0:m, t:t + 1], in1=bias[i][0:m, :],
                        op0=ALU.mult, op1=ALU.add))
                    flush()
                    wait(DVE, w_free[b], *([work_free[k]] if work_free[k] else []))
                    ready = dve.mark(DVE.tensor_scalar(scaled[k][0:m, :], work[k][0:m, :], 0.0, dscale[0:m, t:t + 1],
                                                       ALU.max, ALU.mult))
                    shaped[k] = [ready]
                    wait(ACTE, ready)
                    lows.append((t, act.mark(ACTE.activation(nodes_next[0:m, t, 0, :], scaled[k][0:m, :], ACT.Copy))))

                def flush():
                    while lows:
                        t, high = lows.pop()
                        m, k = rows(t), t % 2
                        wait(DVE, high)
                        new[t] = dve.mark(DVE.tensor_tensor(nodes_next[0:m, t, 1, :], scaled[k][0:m, :],
                                                            nodes_next[0:m, t, 0, :], ALU.subtract))
                        work_free[k] = new[t]

                return start, tile, finish, flush

            table2 = {}
            start, tile, finish, flush = relu_tiles(0, node_b, table2)

            def start_steps():
                wait(ACTE, scale_step())
                start()

            def early_chunk(c):
                first = c * CHUNK // P
                sums = (flat_b[:, c * 2 * HALVES * CHUNK:(c + 1) * 2 * HALVES * CHUNK].bitcast(F32)
                        .rearrange("p (f k) -> p f k", f=HALVES))

                def step():
                    tiles = range(first, first + CHUNK // P)
                    done = [conv_tile(0, t, (t - first) * P, [early_here[c]], weights_in[0], sums) for t in tiles]
                    wait(ACTE, pe.last)
                    wait(DVE, pe.last)
                    for t, (b, product_here) in zip(tiles, done):
                        finish(t, b, product_here)
                    flush()
                return step

            first_layer(node_a, table, 1.0 / SCALE1, [early_chunk(c) for c in range(EARLY)], by_tile(tile, flush),
                        start_steps)

            wait(SP, pe.last)
            weights_in.append(dma("w2_in", SP, weight[0][:, :, :], convs[2][0].rearrange("(f p) d -> p f d", p=P)))
            table3 = {}
            start, tile, _, flush = relu_tiles(1, node_a, table3)
            start()
            layer(node_b, table2, TAIL, scales[:, 3:4], by_tile(tile, flush), one_buffer)

            wait(DVE, pe.last, rel_in, seen["scales"])
            wait(ACTE, dve.mark(DVE.memset(node_b[:, T - 1, :, :], 0.0)))
            relation = slice(REL_ROW, REL_ROW + R)
            rel_again = dma("rel_again", SP, xt[0][relation, :], relvec)
            wait(ACTE, rel_again)
            high = act.mark(ACTE.activation(node_b[relation, T - 1, 0, :], xt[0][relation, :], ACT.Copy, scale=scales[relation, 2:3]))
            wait(DVE, high)
            rel_table = dve.mark(DVE.scalar_tensor_tensor(
                out=node_b[relation, T - 1, 1, :], in0=xt[0][relation, :], scalar=scales[relation, 2:3],
                in1=node_b[relation, T - 1, 0, :], op0=ALU.mult, op1=ALU.subtract))
            wait(SP, rel_table)

            x_tile = [xt[0][:, :], xt[1][:, :], weight[1][:, 0, :], weight[1][:, 1, :]]
            x_loads = [stream(f"x_again{k}", 16) for k in range(len(x_tile))]
            x1_stores = [stream(f"x1_out{k}", 16) for k in range(len(x_tile))]
            x_here, x1_read = {}, {}
            table4 = {}
            order_of = {t: i for i, t in enumerate(order)}

            def load_x(i):
                t, k = order[i], i % len(x_tile)
                wait(SP, *x1_read.get(i - len(x_tile), []))
                x_here[t] = x_loads[k].mark(SP.dma_start(x_tile[k][0:rows(t), :], x[t * P:t * P + rows(t), :]))

            def norm_steps(c, sums, halves):
                tiles = [t for t in order if t * P // CHUNK == c]
                first, end = tiles[0], tiles[-1] + 1
                cols = slice(first, end)
                x1 = {t: x_tile[order_of[t] % len(x_tile)][0:rows(t), :] for t in tiles}

                def step():
                    stored = {}
                    done, x1_here, stats_here = {}, {}, {}
                    for t in tiles:
                        done[t] = conv_tile(2, t, t * P - c * CHUNK, halves, weights_in[2])
                    wait(DVE, dve.last, act.last)
                    for t in tiles:
                        m, k = rows(t), t % 2
                        b, product_here = done[t]
                        wait(DVE, product_here)
                        w_free[b] = dve.mark(DVE.scalar_tensor_tensor(
                            out=work[k][0:m, :], in0=ps[0:m, b, 0:D], scalar=dinv[0:m, t:t + 1], in1=bias[2][0:m, :],
                            op0=ALU.mult, op1=ALU.add))
                        wait(DVE, w_free[b], x_here[t])
                        x1_here[t] = dve.mark(DVE.tensor_tensor(x1[t], x1[t], work[k][0:m, :], ALU.add))
                        wait(SP, x1_here[t])
                        stored[t] = x1_stores[order_of[t] % len(x_tile)].mark(
                            SP.dma_start(x1_dram[t * P:t * P + m, :], x1[t]))
                        wait(DVE, x1_here[t])
                        wait(DVE, dve.mark(DVE.bn_stats(stats[0:m, k, :], x1[t])))
                        wait(DVE, dve.mark(DVE.bn_aggr(moments[0:m, t, :], stats[0:m, k, :])))
                    wait(DVE, dve.mark(DVE.tensor_scalar(newt[:, 3, cols], moments[:, cols, 1], EPS, None, ALU.add)))
                    inverse_root(newt[:, 3, cols], rstd[:, cols], [newt[:, i, cols] for i in range(3)])
                    wait(DVE, dve.last)
                    wait(DVE, dve.mark(DVE.scalar_tensor_tensor(out=negmr[:, cols], in0=moments[:, cols, 0], scalar=-1.0,
                                                                in1=rstd[:, cols], op0=ALU.mult, op1=ALU.mult)))
                    for n, of in enumerate((rstd, negmr)):
                        ready = dve.mark(DVE.tensor_scalar(newt[:, n, cols], of[:, cols], scales[:, 2:3], None, ALU.mult))
                    wait(ACTE, ready)
                    for t in tiles:
                        m, k = rows(t), t % 2
                        if work_free[k]:
                            wait(ACTE, work_free[k])
                        shaped = act.mark(ACTE.activation(scaled[k][0:m, :], x1[t], ACT.Relu,
                                                          bias=newt[0:m, 1, t:t + 1], scale=newt[0:m, 0, t:t + 1]))
                        x1_read[order_of[t]] = [shaped, stored[t]]
                        wait(ACTE, shaped)
                        high = act.mark(ACTE.activation(node_b[0:m, t, 0, :], scaled[k][0:m, :], ACT.Copy))
                        wait(DVE, high)
                        table4[t] = dve.mark(DVE.tensor_tensor(node_b[0:m, t, 1, :], scaled[k][0:m, :],
                                                               node_b[0:m, t, 0, :], ALU.subtract))
                        work_free[k] = table4[t]
                    for t in tiles:
                        if order_of[t] + len(x_tile) < T:
                            load_x(order_of[t] + len(x_tile))
                return [step]

            for i in range(len(x_tile)):
                load_x(i)

            def take_loops_out():
                wait(DVE, pe.last)
                loops_out.append(loops(ALU.subtract))

            loops_out = []
            layer(node_a, table3, TAIL, scales[:, 4:5], norm_steps, one_buffer, at_end=take_loops_out)

            wait(PE, *loops_out)
            gru = gru_setup("", [s.last for s in x1_stores], order)

            def gru_step(t, at_col, sums, halves):
                gru(order_of[t], [sums[f][:, at_col:at_col + rows(t)] for f in range(HALVES)], halves)

            def gru_steps(c, sums, halves):
                return [lambda t=t: gru_step(t, t * P - c * CHUNK, sums, halves) for t in order if t * P // CHUNK == c]

            two_buffers = one_buffer + [[weight[f][:, :, :].rearrange("p f d -> p (f d)") for f in range(HALVES)]]
            layer(node_b, table4, REL_ROW + R, scales[:, 5:6], gru_steps, two_buffers, [pe.last, dve.last])

        for s, n in zip(streams, counted):
            s.n = n

        with nc.Else():
            def settle(*engines, also=()):
                for engine in engines:
                    wait(engine, pe.last, dve.last, act.last, *also)

            at[0] = 0
            node_iota = early(N)
            hot = early(N)
            sums = early(HALVES * N).rearrange("p (f n) -> p f n", f=HALVES)
            message = early(D)
            relation_row = early(D)
            source_id, target_id, relation_id = (early(1, I32) for _ in range(3))
            ones_g, zeros_g = early(P), early(BANK)
            node_iota_i = hot.bitcast(I32)
            a32, b32 = (n[:, :, :, :].rearrange("p t a d -> p (t a d)").bitcast(F32).rearrange("p (t d) -> p t d", t=T)
                        for n in (node_a, node_b))
            totals, mean, squares, factors = norm_x()
            for step in [*totals, mean, *squares, *factors]:
                step()
            settle(ACTE)
            for t in range(T):
                m = rows(t)
                act.mark(ACTE.activation(h1[0:m, t, :], h1[0:m, t, :], ACT.Relu, bias=negmr[0:m, t:t + 1],
                                         scale=rstd[0:m, t:t + 1]))
            settle(POOL, DVE, also=[pool.last, rel_in, *biases_in, *weights_in[:2]])
            numbered = pool.mark(POOL.iota(node_iota_i, pattern=[[1, N]], base=0, channel_multiplier=0))
            wait(DVE, numbered)
            dve.mark(DVE.tensor_copy(node_iota, node_iota_i))
            dve.mark(DVE.memset(ones_g, 1.0))
            dve.mark(DVE.memset(zeros_g, 0.0))
            settle(DVE, PE)

            def handoff(name):
                return ctx.enter_context(nc.semaphore(name))

            def take(engine, sem, n):
                engine.wait_ge(sem, n)
                engine.sem_inc(sem, -n)

            source_here, target_here, relation_here = handoff("source_here"), handoff("target_here"), handoff("relation_here")
            gathered = {}
            hot_here, block_done = handoff("hot_here"), handoff("block_done")
            EDGE_BLOCKS, EDGES_LEFT = E // P, E % P

            def banks():
                return [(c, c * BANK, min(BANK, N - c * BANK)) for c in range(-(-N // BANK))]

            def each_edge_block(products, table=None, relations=False):
                message_here, relation_row_here = gathered.get("now", (None, None))

                def block(k, ids, i):
                    SP.dma_start(target_id[0:k, :], ids(dst)).then_inc(target_here, 16)
                    take(DVE, target_here, 16)
                    DVE.tensor_scalar(hot[0:k, :], node_iota[0:k, :], target_id[0:k, :], None, ALU.is_equal).then_inc(hot_here, 1)
                    if table is not None:
                        SP.dma_start(source_id[0:k, :], ids(src)).then_inc(source_here, 16)
                        take(POOL, source_here, 16)
                        POOL.indirect_dma_start(out=message[0:k, :], out_offset=None, in_=table,
                                                in_offset=bass.IndirectOffsetOnAxis(ap=source_id[0:k, 0:1], axis=0)
                                                ).then_inc(message_here.sem, 16)
                        PE.wait_ge(message_here.sem, i * 16 + (message_here.n + 16))
                    if relations:
                        SP.dma_start(relation_id[0:k, :], ids(rel)).then_inc(relation_here, 16)
                        take(POOL, relation_here, 16)
                        POOL.indirect_dma_start(out=relation_row[0:k, :], out_offset=None, in_=relvec,
                                                in_offset=bass.IndirectOffsetOnAxis(ap=relation_id[0:k, 0:1], axis=0)
                                                ).then_inc(relation_row_here.sem, 16)
                        PE.wait_ge(relation_row_here.sem, i * 16 + (relation_row_here.n + 16))
                    take(PE, hot_here, 1)
                    products(k).then_inc(block_done, 1)
                    take(SP, block_done, 1)

                with nc.Fori(0, EDGE_BLOCKS) as i:
                    block(P, lambda v: v[0:EDGE_BLOCKS * P].rearrange("(b p) -> b p", p=P)[bass.ds(i, 1), :]
                          .rearrange("b p -> p b"), i)
                if EDGES_LEFT:
                    block(EDGES_LEFT, lambda v: v[EDGE_BLOCKS * P:E].rearrange("(p b) -> p b", b=1), EDGE_BLOCKS)
                blocks = EDGE_BLOCKS + (EDGES_LEFT > 0)
                if table is not None:
                    message_here.n += 16 * blocks
                if relations:
                    relation_row_here.n += 16 * blocks

            def clear(bank, cols):
                return pe.mark(PE.matmul(ps[:, bank, 0:cols], zeros_g[:, 0:P], zeros_g[:, 0:cols], start=True, stop=False,
                                         skip_group_check=True))

            clear(0, T)

            def count_block(k):
                for t in range(T):
                    m = rows(t)
                    last = PE.matmul(ps[0:m, 0, t:t + 1], hot[0:k, t * P:t * P + m], ones_g[0:k, 0:1], start=False,
                                     stop=False, skip_group_check=True)
                return last

            each_edge_block(count_block)
            pe.mark(PE.matmul(ps[:, 0, 0:T], zeros_g[:, 0:P], zeros_g[:, 0:T], start=False, stop=True, skip_group_check=True))
            settle(DVE)
            dve.mark(DVE.tensor_scalar(newt[:, 3, :], ps[:, 0, 0:T], 1.0, None, ALU.add))
            wait(DVE, dve.last)
            inverse_root(newt[:, 3, :], dinv[:, :], [newt[:, i, :] for i in range(3)])
            settle(DVE, ACTE)
            for t in range(T):
                dve.mark(DVE.tensor_scalar(a32[0:rows(t), t, :], a32[0:rows(t), t, :], dinv[0:rows(t), t:t + 1], None,
                                           ALU.mult))
            table_out = stream("table_out", 16)

            def sum_all(nodes, loops, relations):
                gathered["now"] = stream(f"message_here{table_out.n}", 16), stream(f"relation_row_here{table_out.n}", 16)
                settle(SP, also=[table_out.last])
                table_out.mark(SP.dma_start(table_dram[0:(T - 1) * P, :].rearrange("(t p) d -> p t d", p=P),
                                            nodes[:, 0:T - 1, :]))
                table_out.mark(SP.dma_start(table_dram[(T - 1) * P:N, :], nodes[0:TAIL, T - 1, :]))
                wait(POOL, table_out.last)
                for f in range(HALVES):
                    settle(PE, also=[table_out.last])
                    for c, _, cols in banks():
                        clear(c, cols)
                    settle(DVE)

                    def sum_block(k):
                        for rows_of in (message, relation_row)[:2 if relations else 1]:
                            for c, start, cols in banks():
                                last = PE.matmul(ps[:, c, 0:cols], rows_of[0:k, f * P:(f + 1) * P], hot[0:k, start:start + cols],
                                                 start=False, stop=False, skip_group_check=True)
                        return last

                    each_edge_block(sum_block, table_dram, relations)
                    if loops:
                        for t in range(T):
                            m, c = rows(t), t * P // BANK
                            PE.matmul(ps[:, c, t * P - c * BANK:t * P - c * BANK + m], nodes[0:m, t, f * P:(f + 1) * P],
                                      ident[0:m, 0:m], start=False, stop=False, skip_group_check=True)
                    for c, _, cols in banks():
                        pe.mark(PE.matmul(ps[:, c, 0:cols], zeros_g[:, 0:P], zeros_g[:, 0:cols], start=False, stop=True,
                                          skip_group_check=True))
                    settle(DVE)
                    for c, start, cols in banks():
                        dve.mark(DVE.tensor_copy(sums[:, f, start:start + cols], ps[:, c, 0:cols]))

            def product_tile(t, w):
                settle(PE)
                for f in range(HALVES):
                    last = PE.matmul(ps[0:rows(t), 7, 0:D], sums[:, f, t * P:t * P + rows(t)], w[:, f, :], start=(f == 0),
                                     stop=(f == HALVES - 1))
                return pe.mark(last)

            for i, (nodes, following) in enumerate(((a32, b32), (b32, a32))):
                sum_all(nodes, True, False)
                for t in range(T):
                    m, k = rows(t), t % 2
                    product_tile(t, weight[i])
                    settle(DVE)
                    wait(DVE, dve.mark(DVE.scalar_tensor_tensor(
                        out=work[k][0:m, :], in0=ps[0:m, 7, 0:D], scalar=dinv[0:m, t:t + 1], in1=bias[i][0:m, :],
                        op0=ALU.mult, op1=ALU.add)))
                    dve.mark(DVE.tensor_scalar(following[0:m, t, :], work[k][0:m, :], 0.0, dinv[0:m, t:t + 1],
                                               ALU.max, ALU.mult))
            sum_all(a32, True, False)
            settle(SP)
            w3_here = dma("w2_in_g", SP, weight[0][:, :, :], convs[2][0].rearrange("(f p) d -> p f d", p=P))
            wait(PE, w3_here)
            streams_g = [stream(f"x_again_g{k}", 16) for k in range(2)], [stream(f"x1_out_g{k}", 16) for k in range(2)]
            x_read_g = {}
            for t in range(T):
                m, k = rows(t), t % 2
                done = product_tile(t, weight[0])
                settle(SP)
                residual_tile(t, 7, done, streams_g, x_read_g)
                settle(ACTE)
                act.mark(ACTE.activation(b32[0:m, t, :], xt[k][0:m, :], ACT.Relu, bias=negmr[0:m, t:t + 1],
                                         scale=rstd[0:m, t:t + 1]))
                x_read_g[k].append(act.last)
            sum_all(b32, False, True)
            gru_g = gru_setup("g_", [s.last for s in streams_g[1]] + [table_out.last], range(T))
            for t in range(T):
                settle(PE)
                gru_g(t, [sums[:, f, t * P:t * P + rows(t)] for f in range(HALVES)], [])


_INPUTS = ("x", "src", "dst", "edge_type_16", "L0_gnn_W1", "L0_gnn_b1", "L0_gnn_W2", "L0_gnn_b2", "L0_gnn_W3",
           "L0_gnn_b3", "L1_gnn_relvectors", "L1_gnn_w_ih", "L1_gnn_w_hh", "L1_gnn_b_ih", "L1_gnn_b_hh")


def kernel(**inputs):
    import numpy as np
    import concourse.bacc as bacc
    from concourse import mybir as mb
    from concourse.bass_utils import run_bass_kernel_spmd

    nc = bacc.Bacc("TRN2", target_bir_lowering=False, num_devices=1, dynamic_dma_scratch_size=1024)
    arrays, ap = {}, {}
    for name in _INPUTS:
        a = np.asarray(inputs[name])
        if name in ("L1_gnn_w_ih", "L1_gnn_w_hh"):
            a = a.T
        a = np.ascontiguousarray(a)
        arrays[f"in_{name}"] = a
        ap[name] = nc.dram_tensor(f"in_{name}", a.shape, mb.dt.from_np(a.dtype), kind="ExternalInput").ap()
    shape = tuple(arrays["in_x"].shape)
    out = nc.dram_tensor("out_0", shape, mb.dt.float32, kind="ExternalOutput").ap()
    x1 = nc.dram_tensor("x1_scratch", shape, mb.dt.float32, kind="Internal").ap()
    table = nc.dram_tensor("table_scratch", shape, mb.dt.float32, kind="Internal").ap()
    convs = [(ap[f"L0_gnn_W{i}"], ap[f"L0_gnn_b{i}"]) for i in (1, 2, 3)]
    program(nc, ap["x"], ap["src"], ap["dst"], ap["edge_type_16"], convs, ap["L1_gnn_relvectors"], ap["L1_gnn_w_ih"],
            ap["L1_gnn_w_hh"], ap["L1_gnn_b_ih"], ap["L1_gnn_b_hh"], x1, table, out)
    result = run_bass_kernel_spmd(nc, [arrays], core_ids=[0])
    return result.results[0]["out_0"]
```
